# Optimizing a Trainium2 kernel written in Bass

```python
import numpy as np
import jax
import jax.numpy as jnp

def _softmax(x, axis=-1):
    return jax.nn.softmax(x, axis=axis)

def _gelu(x):
    return jax.nn.gelu(x, approximate=True)

def _silu(x):
    return jax.nn.silu(x)

def _sigmoid(x):
    return jax.nn.sigmoid(x)

def _layernorm(x, axis=-1, eps=1e-05):
    m = jnp.mean(x, axis=axis, keepdims=True)
    v = jnp.var(x, axis=axis, keepdims=True)
    return (x - m) / jnp.sqrt(v + eps)

def _scatter_add(tgt, idx, src, axis=0):
    return tgt.at[idx].add(src)

def _segment_sum(src, seg, n):
    return jax.ops.segment_sum(src, seg, n)
kernel_name = 'mk_prb_d1_jaxref_r8_58dbd1'

def setup_inputs(seed: int=0):
    np.random.seed(seed)
    _w = jnp.asarray

    def _L0_attn_setup():
        import jax, jax.numpy as jnp
        import numpy as np
        import math
        H = 16
        EPS = 1e-05
        key = jax.random.key(seed)
        ks = jax.random.split(key, 4)
        B, T, D = (2, 256, 128)
        s = 1.0 / math.sqrt(D)
        return {'x': jax.random.normal(ks[0], (B, T, D), dtype=jnp.float32), 'ln_g': jnp.ones((D,), jnp.float32), 'ln_b': jnp.zeros((D,), jnp.float32), 'Wq': jax.random.normal(ks[1], (D, D), jnp.float32) * s, 'bq': jnp.zeros((D,), jnp.float32), 'Wk': jax.random.normal(ks[2], (D, D), jnp.float32) * s, 'bk': jnp.zeros((D,), jnp.float32), 'Wv': jax.random.normal(ks[3], (D, D), jnp.float32) * s, 'bv': jnp.zeros((D,), jnp.float32)}
    _L0_attn_in = _L0_attn_setup()

    def _L0_ffn_setup():
        import jax, jax.numpy as jnp
        import numpy as np
        B, S, DIM = (2, 256, 128)
        HID = 256
        E, NSH, TOPK = (8, 2, 2)

        def _ffn(x, w1, w2, w3):
            return jax.nn.silu(x @ w1.T) * (x @ w3.T) @ w2.T
        key = jax.random.key(seed)
        ks = jax.random.split(key, 8)
        sc = 0.02
        return {'x': jax.random.normal(ks[0], (B, S, DIM), jnp.float32), 'router_w': jax.random.normal(ks[1], (E, DIM), jnp.float32) * sc, 'expert_bias': jnp.zeros((E,), jnp.float32), 'w1': jax.random.normal(ks[2], (E, HID, DIM), jnp.float32) * sc, 'w3': jax.random.normal(ks[3], (E, HID, DIM), jnp.float32) * sc, 'w2': jax.random.normal(ks[4], (E, DIM, HID), jnp.float32) * sc, 'sw1': jax.random.normal(ks[5], (NSH, HID, DIM), jnp.float32) * sc, 'sw3': jax.random.normal(ks[6], (NSH, HID, DIM), jnp.float32) * sc, 'sw2': jax.random.normal(ks[7], (NSH, DIM, HID), jnp.float32) * sc}
    _L0_ffn_in = _L0_ffn_setup()
    _d = {'L0_attn_x': _L0_attn_in['x'], 'L0_attn_ln_g': _L0_attn_in['ln_g'], 'L0_attn_ln_b': _L0_attn_in['ln_b'], 'L0_attn_Wq': _L0_attn_in['Wq'], 'L0_attn_bq': _L0_attn_in['bq'], 'L0_attn_Wk': _L0_attn_in['Wk'], 'L0_attn_bk': _L0_attn_in['bk'], 'L0_attn_Wv': _L0_attn_in['Wv'], 'L0_attn_bv': _L0_attn_in['bv'], 'L0_ffn_router_w': _L0_ffn_in['router_w'], 'L0_ffn_expert_bias': _L0_ffn_in['expert_bias'], 'L0_ffn_w1': _L0_ffn_in['w1'], 'L0_ffn_w3': _L0_ffn_in['w3'], 'L0_ffn_w2': _L0_ffn_in['w2'], 'L0_ffn_sw1': _L0_ffn_in['sw1'], 'L0_ffn_sw3': _L0_ffn_in['sw3'], 'L0_ffn_sw2': _L0_ffn_in['sw2']}
    _x0 = _d['L0_attn_x']
    _d['L0_attn_x'] = jax.random.normal(jax.random.fold_in(jax.random.key(seed), 1), (16, 512, 128), dtype=_x0.dtype)
    del _x0
    return _d

def reference(L0_attn_x, L0_attn_ln_g, L0_attn_ln_b, L0_attn_Wq, L0_attn_bq, L0_attn_Wk, L0_attn_bk, L0_attn_Wv, L0_attn_bv, L0_ffn_router_w, L0_ffn_expert_bias, L0_ffn_w1, L0_ffn_w3, L0_ffn_w2, L0_ffn_sw1, L0_ffn_sw3, L0_ffn_sw2):

    def _L0_attn_ref(x, ln_g, ln_b, Wq, bq, Wk, bk, Wv, bv):
        import jax, jax.numpy as jnp
        import numpy as np
        import math
        H = 16
        EPS = 1e-05
        B, T, D = x.shape
        mu = jnp.mean(x, axis=-1, keepdims=True)
        var = jnp.mean(jnp.square(x - mu), axis=-1, keepdims=True)
        xn = (x - mu) * jax.lax.rsqrt(var + EPS) * ln_g + ln_b
        q = (xn @ Wq + bq).reshape(B, T, H, D // H)
        k = (xn @ Wk + bk).reshape(B, T, H, D // H)
        v = (xn @ Wv + bv).reshape(B, T, H, D // H)
        scale = 1.0 / math.sqrt(D // H)
        attn = jnp.einsum('bnhd,bmhd->bnmh', q, k) * scale
        w = jax.nn.softmax(attn, axis=2)
        y = jnp.einsum('bnmh,bmhd->bnhd', w, v).reshape(B, T, D)
        return y

    def _L0_ffn_ref(x, router_w, expert_bias, w1, w3, w2, sw1, sw3, sw2):
        import jax, jax.numpy as jnp
        import numpy as np
        B, S, DIM = (2, 256, 128)
        HID = 256
        E, NSH, TOPK = (8, 2, 2)

        def _ffn(x, w1, w2, w3):
            return jax.nn.silu(x @ w1.T) * (x @ w3.T) @ w2.T
        bs, sl, d = x.shape
        xf = x.reshape(-1, d)
        shared = jnp.zeros_like(xf)
        for i in range(sw1.shape[0]):
            shared = shared + _ffn(xf, sw1[i], sw2[i], sw3[i])
        logits = xf @ router_w.T + expert_bias
        rw, sel = jax.lax.top_k(logits, TOPK)
        rw = jax.nn.softmax(rw.astype(jnp.float32), axis=-1).astype(x.dtype)
        onehot = jax.nn.one_hot(sel, E, dtype=x.dtype)
        combine = jnp.einsum('tk,tke->te', rw, onehot)

        def body(acc, ew):
            e1, e3, e2, cw = ew
            acc = acc + cw[:, None] * _ffn(xf, e1, e2, e3)
            return (acc, None)
        out, _ = jax.lax.scan(body, jnp.zeros_like(xf), (w1, w3, w2, combine.T))
        out = out + shared
        return out.reshape(bs, sl, -1)
    x = L0_attn_x
    xn = _layernorm(x, axis=-1)
    x = x + _L0_attn_ref(xn, L0_attn_ln_g, L0_attn_ln_b, L0_attn_Wq, L0_attn_bq, L0_attn_Wk, L0_attn_bk, L0_attn_Wv, L0_attn_bv) + _L0_ffn_ref(xn, L0_ffn_router_w, L0_ffn_expert_bias, L0_ffn_w1, L0_ffn_w3, L0_ffn_w2, L0_ffn_sw1, L0_ffn_sw3, L0_ffn_sw2)
    return x

_drawn_inputs = setup_inputs


def setup_inputs(seed=0):
    import zlib

    import numpy as np

    out = dict(_drawn_inputs(seed))
    spreads = {'L0_attn_ln_g': (1.0, 0.6),
     'L0_attn_ln_b': (0.0, 0.391),
     'L0_attn_bq': (0.0, 2.0),
     'L0_attn_bk': (0.0, 2.0),
     'L0_attn_bv': (0.0, 0.401),
     'L0_ffn_expert_bias': (0.0, 0.8)}
    factors = {'L0_ffn_router_w': 8.0,
     'L0_ffn_w1': 8.0,
     'L0_ffn_w3': 8.0,
     'L0_ffn_w2': 8.0,
     'L0_ffn_sw1': 4.926,
     'L0_ffn_sw3': 4.899,
     'L0_ffn_sw2': 4.91}
    for name, (base, spread) in spreads.items():
        noise = np.random.default_rng([zlib.crc32(name.encode()), seed]).standard_normal(out[name].shape)
        drawn = base * np.exp(spread * noise) if base else spread * noise
        out[name] = jnp.asarray(drawn.astype(out[name].dtype))
    for name, factor in factors.items():
        out[name] = (out[name] * factor).astype(out[name].dtype)
    return out
```

```python
from contextlib import ExitStack

import concourse.bass as bass
from concourse import mybir

F32 = mybir.dt.float32
F32R = mybir.dt.float32r
ALU = mybir.AluOpType
ACT = mybir.ActivationFunctionType
AX_X = mybir.AxisListType.X

P = 128
EPS = 1e-5
TERMS = 4
GROUP = 4
HI_SLOTS_Q = (0, 1)
LO_SLOT_Q = 2
HI_SLOTS_K = (0, 2)
LO_SLOT_K = 1
SHIFT_SLOT = 3
PROBS_RING = 4
BANKS = 3
FAR_BELOW = -3.0e38


def prenorm_attention_moe(nc, x, vecs, wqkv, experts, router, router_bias, rank, ident_in, out):
    B, T, D = x.shape
    E = router.shape[1]
    NE = experts.shape[1]
    HID = experts.shape[2] // 3
    NB = T // P
    HC = HID // P
    HEADS = 16
    DH = D // HEADS
    GROUPS = HEADS // GROUP
    SCALE = float(DH) ** -0.5
    ROWS = DH * TERMS
    G_ALL = B * GROUPS
    assert D == P and ROWS * GROUP == P and T == 512 and B % 2 == 0 and GROUPS == 4 and NB == 4

    xnT_dram = nc.dram_tensor("xnT_dram", [B, P, T], F32, kind="Internal").ap()
    attn_dram = nc.dram_tensor("attn_dram", [B, P, NB, D], F32, kind="Internal").ap()
    combine_dram = nc.dram_tensor("combine_dram", [B * NB * E, P], F32, kind="Internal").ap()

    with ExitStack() as outer:
        def keep(name, shape, dt):
            return outer.enter_context(nc.sbuf_tensor(name, shape, dt))

        ident = keep("ident", [P, P], F32)
        w_hi = keep("w_hi", [P, NE, 3 * HID], F32R)
        w_lo = keep("w_lo", [P, NE, 3 * HID], F32R)
        attention_block(nc, locals())
        router_block(nc, locals())
        experts_block(nc, locals())


def attention_block(nc, env):
    x, vecs, wqkv, experts, ident_in = (env[k] for k in ("x", "vecs", "wqkv", "experts", "ident_in"))
    B, T, D, NB, NE, HID, DH, HEADS, GROUPS, ROWS, G_ALL, SCALE = (
        env[k] for k in ("B", "T", "D", "NB", "NE", "HID", "DH", "HEADS", "GROUPS", "ROWS", "G_ALL", "SCALE"))
    xnT_dram, attn_dram, ident, w_hi, w_lo = (env[k] for k in ("xnT_dram", "attn_dram", "ident", "w_hi", "w_lo"))
    LAST_PREP = B - 2

    with ExitStack() as ctx:
        def sb(name, shape, dt):
            return ctx.enter_context(nc.sbuf_tensor(name, shape, dt))

        def sem(name):
            return ctx.enter_context(nc.semaphore(name))

        vec = sb("vec", [P, 5], F32)
        bq_scaled = sb("bq_scaled", [P, 1], F32)
        small = sb("small", [P, 4, NB], F32)
        w_stage = sb("w_stage", [P, 3 * HID], F32)
        wp_raw = sb("wp_raw", [P, 3, D], F32)
        wp_hi = sb("wp_hi", [P, 3, D], F32R)
        wp_lo = sb("wp_lo", [P, 3, D], F32R)
        x_in = sb("x_in", [P, 2, NB, D], F32)
        bn = sb("bn", [P, NB, 6], F32)
        moments = sb("moments", [P, NB, 2], F32)
        coef = sb("coef", [P, 8, NB], F32)
        xn = sb("xn", [P, NB, D], F32)
        xa = sb("xa", [P, NB, D], F32)
        xnT = sb("xnT", [P, T], F32)
        xaT = sb("xaT", [P, T], F32)
        xaT_hi = sb("xaT_hi", [P, T], F32R)
        xaT_lo = sb("xaT_lo", [P, T], F32R)
        qT = sb("qT", [P, T], F32)
        kT = sb("kT", [P, T], F32)
        vT = sb("vT", [P, T], F32)
        q_terms = sb("q_terms", [P, 2, TERMS, T], F32R)
        k_terms = sb("k_terms", [P, 2, TERMS, T], F32R)
        q_stack = sb("q_stack", [P, GROUPS, GROUP, T], F32R)
        k_stack = sb("k_stack", [P, GROUPS, T], F32R)
        v_one = sb("v_one", [P, 2, NB, HEADS, DH + 1], F32)
        maxima = sb("maxima", [P, 2, GROUP * NB], F32)
        shift = sb("shift", [GROUP * NB, 2, P], F32R)
        probs = sb("probs", [P, PROBS_RING, GROUP, T], F32)
        oT = sb("oT", [P, T], F32)
        recip = sb("recip", [P, NB, GROUP], F32)
        attn = sb("attn", [P, 2, NB, D], F32)

        ps_scores = ctx.enter_context(nc.psum_tensor("ps_scores", [P, BANKS, T], F32))
        ps_scoresT = ctx.enter_context(nc.psum_tensor("ps_scoresT", [P, BANKS, T], F32))
        ps_out = ctx.enter_context(nc.psum_tensor("ps_out", [P, T], F32))
        ps_misc = ctx.enter_context(nc.psum_tensor("ps_misc", [P, T], F32))

        params_loaded = sem("params_loaded")
        consts_ready = sem("consts_ready")
        pool_consts = sem("pool_consts")
        x_loaded = [sem("x_loaded0"), sem("x_loaded1")]
        bn_done = sem("bn_done")
        moments_ready = sem("moments_ready")
        coef_step = sem("coef_step")
        normed = sem("normed")
        misc_filled = sem("misc_filled")
        misc_emptied = sem("misc_emptied")
        xa_hi_ready = sem("xa_hi_ready")
        xa_lo_ready = sem("xa_lo_ready")
        hi_terms = sem("hi_terms")
        lo_terms = sem("lo_terms")
        stacks_loaded = [sem(f"stacks_loaded{g}") for g in range(GROUPS)]
        scores_ready = sem("scores_ready")
        maxima_ready = sem("maxima_ready")
        shift_loaded = sem("shift_loaded")
        scoresT_ready = sem("scoresT_ready")
        probs_ready = sem("probs_ready")
        pv_done = sem("pv_done")
        oT_ready = sem("oT_ready")
        recip_ready = sem("recip_ready")
        xnT_stored = sem("xnT_stored")
        attn_stored = sem("attn_stored")
        w_loaded = sem("w_loaded")
        w_hi_done = sem("w_hi_done")
        w_lo_done = sem("w_lo_done")

        PARAM_DMAS = 3
        COEFS = 8
        NORMED = NB + 1
        block = ctx.enter_context(nc.Block())

        LEAD_USES = 12
        PREP_BEFORE = (0, 1, 3, 5)

        def misc_before(b, g):
            if not isinstance(b, int):
                return b * (2 * GROUPS + 6) + (LEAD_USES + 2 * g - 1 + PREP_BEFORE[g])
            G = b * GROUPS + g
            prep = 6 * min(b, LAST_PREP)
            if b < LAST_PREP:
                prep += PREP_BEFORE[g]
            elif b == LAST_PREP:
                prep += 1 if g else 0
            else:
                prep += 1
            return LEAD_USES + max(G - 1, 0) + min(G, G_ALL - 1) + prep

        def use_m(b, g):
            return misc_before(b, g)

        def use_t(b, g):
            last = isinstance(b, int) and b == B - 1 and g == GROUPS - 1
            return misc_before(b, g) + (0 if last else 1)

        def use_prep(b, g, n):
            first = isinstance(b, int) and b == 0 and g == 0
            return misc_before(b, g) + (1 if first else 2) + n

        def use_xn(n, ahead):
            return (0, 6)[ahead] if ahead in (0, 1) else use_prep(n - 2, 1, 0)

        def use_of(kind, n):
            lead = {"xn": 0, "xa": 1, "q": 2, "k": 3, "v": 4, "vt": 5}[kind]
            if isinstance(n, int) and n == 0:
                return lead
            if kind == "vt":
                return use_prep(n - 1, 0, 0)
            if isinstance(n, int) and n == 1:
                return 6 + lead
            g, k = {"xn": (1, 0), "xa": (1, 1), "q": (2, 0), "k": (2, 1), "v": (3, 0)}[kind]
            return use_prep(n - 2, g, k)

        def bank(g, par, k):
            ring = 2 * GROUPS * GROUP * NB
            at = (par * GROUPS + g) * GROUP * NB + k
            if at >= BANKS:
                return at % BANKS, BANKS
            last = max(v for v in range(ring) if v % BANKS == at)
            return at, at + ring - last

        def batches(eng, body):
            body(0, 0)
            body(1, 1)
            with eng.Fori(1, B // 2 - 1) as pair:
                body(pair * 2, 0)
                body(pair * 2 + 1, 1)
            body(B - 2, 0)
            body(B - 1, 1)

        def at_start(b, g=0):
            return isinstance(b, int) and b == 0 and g == 0

        def at_end(b, g=3):
            return isinstance(b, int) and b == B - 1 and g == GROUPS - 1

        def prepares(b):
            return not isinstance(b, int) or b < LAST_PREP

        def has_next(b):
            return not isinstance(b, int) or b < B - 1

        def half(b, par):
            return b // 2 if isinstance(b, int) else (b - par) // 2

        @block.sync
        def _(sp):
            sp.dma_start(x_in[:, 0], x[0].rearrange("(n p) d -> p n d", p=P)).then_inc(x_loaded[0], 16)
            sp.dma_start(vec[:, :], vecs).then_inc(params_loaded, 16)
            sp.dma_start(ident[:, :], ident_in).then_inc(params_loaded, 16)
            sp.dma_start(wp_raw[:, :, :], wqkv).then_inc(params_loaded, 16)
            sp.dma_start(x_in[:, 1], x[1].rearrange("(n p) d -> p n d", p=P)).then_inc(x_loaded[1], 16)

            def load_x(n, par):
                sp.wait_ge(normed, (n - 1) * NORMED)
                src = x[n] if isinstance(n, int) else x[bass.ds(n, 1)].rearrange("o t d -> (o t) d")
                sp.dma_start(x_in[:, par], src.rearrange("(n p) d -> p n d", p=P)).then_inc(x_loaded[par], 16)

            def store_xnT(n):
                sp.wait_ge(misc_emptied, use_of("xn", n) + 1)
                dst = xnT_dram[n] if isinstance(n, int) else xnT_dram[bass.ds(n, 1)].rearrange("o p t -> (o p) t")
                sp.dma_start(dst, xnT[:, :]).then_inc(xnT_stored, 16)

            def store_attn(n, par, emptied):
                sp.wait_ge(misc_emptied, emptied)
                dst = attn_dram[n] if isinstance(n, int) else attn_dram[bass.ds(n, 1)].rearrange("o p n d -> (o p) n d")
                sp.dma_start(dst, attn[:, par]).then_inc(attn_stored, 16)

            def load_stacks(n, par, g, freed):
                sp.wait_ge(lo_terms, n * 2 + 2)
                if freed is not None:
                    sp.wait_ge(scoresT_ready, freed)
                rows = GROUP * DH
                sp.dma_start(k_stack[:, g, :].bitcast(F32),
                             k_terms[g * rows:(g + 1) * rows, par].bitcast(F32)).then_inc(stacks_loaded[g], 16)
                for j in range(GROUP):
                    h = g * GROUP + j
                    sp.dma_start(q_stack[j * ROWS:(j + 1) * ROWS, g, j, :].bitcast(F32),
                                 q_terms[h * DH:(h + 1) * DH, par].bitcast(F32)).then_inc(stacks_loaded[g], 16)

            def load_shift(g, par, emptied):
                sp.wait_ge(misc_emptied, emptied)
                for j in range(GROUP):
                    row = j * ROWS + SHIFT_SLOT
                    sp.dma_start(q_stack[row:row + 1, g, j, :].bitcast(F32),
                                 shift[j * NB:(j + 1) * NB, par, :].bitcast(F32)).then_inc(shift_loaded, 16)

            store_xnT(0)
            sp.wait_ge(pool_consts, 3)
            for g in range(GROUPS):
                load_stacks(0, 0, g, None)
            store_xnT(1)
            load_shift(0, 0, LEAD_USES)

            def body(b, par):
                for g in range(GROUPS):
                    G = b * GROUPS + g
                    if g == 0 and prepares(b):
                        load_x(b + 2, par)
                    if not at_end(b, g):
                        load_shift((g + 1) % GROUPS, (g + 1) % 2, use_m(b, g) + 1)
                    if g == 0 and not at_start(b):
                        store_attn(b - 1, 1 - par, use_t(b, 0) + 1)
                    if g == 2 and prepares(b):
                        store_xnT(b + 2)
                    if has_next(b):
                        load_stacks(b + 1, 1 - par, g, (G + 1) * (GROUP * NB))

            batches(sp, body)
            store_attn(B - 1, (B - 1) % 2, misc_before(B - 1, GROUPS - 1) + 2)
            sp.wait_ge(xnT_stored, 16 * B)
            sp.wait_ge(attn_stored, 16 * B)

        @block.gpsimd
        def _(pool):
            for k, value in enumerate((-0.5, EPS, -1.0)):
                pool.memset(small[:, k, :], value)
            pool.memset(small[:, 3, :], 0.0).then_inc(pool_consts, 1)
            pool.memset(q_stack[:, :, :, :].bitcast(F32), 0.0).then_inc(pool_consts, 1)
            pool.memset(q_terms[:, :, SHIFT_SLOT, :].bitcast(F32), 0.0)
            pool.memset(k_terms[:, :, SHIFT_SLOT, :].bitcast(F32), 1.0).then_inc(pool_consts, 1)
            pool.wait_ge(pool_consts, 3)

            def normalise(n, par):
                base = n * COEFS
                mean, var = moments[:, :, 0], moments[:, :, 1]
                ve, r, mr, bias, vr, vrr, ve2, r2 = (coef[:, k, :] for k in range(COEFS))
                pool.wait_ge(moments_ready, n * NB + NB)
                if not (isinstance(n, int) and n == 0):
                    pool.wait_ge(normed, n * NORMED)
                pool.tensor_tensor(ve, var, small[:, 1, :], ALU.add).then_inc(coef_step, 1)
                pool.wait_ge(coef_step, base + 1)
                pool.tensor_tensor(r, ve, small[:, 0, :], ALU.pow).then_inc(coef_step, 1)
                pool.wait_ge(coef_step, base + 2)
                pool.tensor_tensor(mr, mean, r, ALU.mult).then_inc(coef_step, 1)
                pool.wait_ge(coef_step, base + 3)
                pool.tensor_tensor(bias, mr, small[:, 2, :], ALU.mult).then_inc(coef_step, 1)
                if not (isinstance(n, int) and n == 0):
                    pool.wait_ge(misc_filled, use_of("xa", n - 1) + 1)
                pool.wait_ge(coef_step, base + 4)
                pool.tensor_tensor(vr, var, r, ALU.mult).then_inc(coef_step, 1)
                for t in range(NB):
                    pool.tensor_scalar(xn[:, t, :], x_in[:, par, t, :], r[:, t:t + 1],
                                       bias[:, t:t + 1], ALU.mult, ALU.add).then_inc(normed, 1)
                pool.wait_ge(coef_step, base + 5)
                pool.tensor_tensor(vrr, vr, r, ALU.mult).then_inc(coef_step, 1)
                pool.wait_ge(coef_step, base + 6)
                pool.tensor_tensor(ve2, vrr, small[:, 1, :], ALU.add).then_inc(coef_step, 1)
                pool.wait_ge(coef_step, base + 7)
                pool.tensor_tensor(r2, ve2, small[:, 0, :], ALU.pow).then_inc(coef_step, 1)
                pool.wait_ge(coef_step, base + 8)
                pool.wait_ge(normed, n * NORMED + NB)
                r2_wide = r2.rearrange("p (n o) -> p n o", o=1).broadcast_to([P, NB, D])
                pool.tensor_tensor(xa[:, :, :], xn[:, :, :], r2_wide, ALU.mult).then_inc(normed, 1)

            def split_xa(n):
                pool.wait_ge(xa_hi_ready, n + 1)
                if not (isinstance(n, int) and n == 0):
                    pool.wait_ge(misc_filled, use_of("v", n - 1) + 1)
                pool.tensor_tensor(xaT_lo[:, :], xaT[:, :], xaT_hi[:, :].bitcast(F32),
                                   ALU.subtract).then_inc(xa_lo_ready, 1)

            def split_qk(n, par):
                pool.wait_ge(hi_terms, n * 2 + 1)
                pool.tensor_tensor(q_terms[:, par, LO_SLOT_Q, :], qT[:, :],
                                   q_terms[:, par, HI_SLOTS_Q[0], :].bitcast(F32), ALU.subtract).then_inc(lo_terms, 1)
                pool.wait_ge(hi_terms, n * 2 + 2)
                pool.tensor_tensor(k_terms[:, par, LO_SLOT_K, :], kT[:, :],
                                   k_terms[:, par, HI_SLOTS_K[0], :].bitcast(F32), ALU.subtract).then_inc(lo_terms, 1)

            for n in range(2):
                normalise(n, n)
                split_xa(n)
                split_qk(n, n)

            def body(b, par):
                if prepares(b):
                    normalise(b + 2, par)
                    split_xa(b + 2)
                    split_qk(b + 2, par)

            batches(pool, body)

            for e in range(NE):
                if e:
                    pool.wait_ge(w_lo_done, e)
                pool.dma_start(w_stage[:, :], experts[:, e, :]).then_inc(w_loaded, 16)
                pool.wait_ge(w_loaded, 16 * (e + 1))
                pool.tensor_copy(w_hi[:, e, :], w_stage[:, :]).then_inc(w_hi_done, 1)
                pool.wait_ge(w_hi_done, e + 1)
                pool.tensor_tensor(w_lo[:, e, :], w_stage[:, :], w_hi[:, e, :].bitcast(F32),
                                   ALU.subtract).then_inc(w_lo_done, 1)
            pool.wait_ge(w_lo_done, NE)

        @block.tensor
        def _(pe):
            def begin(use):
                if not (isinstance(use, int) and use == 0):
                    pe.wait_ge(misc_emptied, use)

            def turn_blocks(use, src):
                begin(use)
                for t in range(NB):
                    last = pe.transpose(ps_misc[:, t * P:(t + 1) * P], src[:, t, :], ident[:, :])
                last.then_inc(misc_filled, 1)

            def prep(kind, n):
                use = use_of(kind, n)
                if kind == "xn":
                    pe.wait_ge(normed, n * NORMED + NB)
                    turn_blocks(use, xn)
                elif kind == "xa":
                    pe.wait_ge(normed, n * NORMED + NORMED)
                    turn_blocks(use, xa)
                elif kind == "vt":
                    pe.wait_ge(misc_emptied, use_of("v", n) + 1)
                    turn_blocks(use, vT[:, :].rearrange("p (n q) -> p n q", q=P))
                else:
                    w = "qkv".index(kind)
                    pe.wait_ge(xa_lo_ready, n + 1)
                    begin(use)
                    pe.matmul(ps_misc[:, :], wp_hi[:, w, :], xaT_hi[:, :], start=True, stop=False)
                    pe.matmul(ps_misc[:, :], wp_hi[:, w, :], xaT_lo[:, :], start=False, stop=False)
                    pe.matmul(ps_misc[:, :], wp_lo[:, w, :], xaT_hi[:, :], start=False,
                              stop=True).then_inc(misc_filled, 1)

            def scores(G, g, par, k):
                j, n = k // NB, k % NB
                at, back = bank(g, par, k)
                if not (isinstance(G, int) and G * 16 + k < BANKS):
                    pe.wait_ge(maxima_ready, G * 16 + (k + 1 - back))
                pe.matmul(ps_scores[:, at, :], q_stack[:, g, j, n * P:(n + 1) * P],
                          k_stack[:, g, :], start=True, stop=True).then_inc(scores_ready, 1)

            def scoresT(G, g, par, k):
                m, j = k // GROUP, k % GROUP
                at, back = bank(g, par, k)
                if not (isinstance(G, int) and G * 16 + k < BANKS):
                    pe.wait_ge(probs_ready, G * 16 + (k + 1 - back))
                pe.matmul(ps_scoresT[:, at, :], k_stack[:, g, m * P:(m + 1) * P],
                          q_stack[:, g, j, :], start=True, stop=True).then_inc(scoresT_ready, 1)

            def values(G, g, par, m):
                pe.wait_ge(probs_ready, G * 16 + (m + 1) * GROUP)
                if m == 0 and not (isinstance(G, int) and G == 0):
                    pe.wait_ge(oT_ready, G)
                for j in range(GROUP):
                    mm = pe.matmul(ps_out[j * ROWS:j * ROWS + DH + 1, :], v_one[:, par, m, g * GROUP + j, :],
                                   probs[:, m, j, :], start=(m == 0), stop=(m == NB - 1),
                                   tile_position=(0, j * ROWS))
                mm.then_inc(pv_done, 1)

            def turn_maxima(use, G, par):
                pe.wait_ge(maxima_ready, G * 16 + 16)
                begin(use)
                pe.transpose(ps_misc[0:GROUP * NB, 0:P], maxima[:, par, :], ident[:, :]).then_inc(misc_filled, 1)

            def turn_output(use, G):
                pe.wait_ge(oT_ready, G + 1)
                turn_blocks(use, oT[:, :].rearrange("p (n q) -> p n q", q=P))

            pe.wait_ge(params_loaded, 16 * PARAM_DMAS)
            pe.wait_ge(consts_ready, 3)
            for kind in ("xn", "xa", "q", "k", "v", "vt"):
                prep(kind, 0)
            for kind in ("xn", "xa", "q", "k", "v"):
                prep(kind, 1)
            for G in range(2):
                pe.wait_ge(stacks_loaded[G], 80)
                for k in range(GROUP * NB):
                    scores(G, G, 0, k)
            turn_maxima(LEAD_USES - 1, 0, 0)

            def body(b, par):
                for g in range(GROUPS):
                    G = b * GROUPS + g
                    ahead = not isinstance(b, int) or G + 2 < G_ALL
                    pe.wait_ge(shift_loaded, G * (16 * GROUP) + 16 * GROUP)
                    if ahead:
                        g2 = (g + 2) % GROUPS
                        pe.wait_ge(stacks_loaded[g2], (b + (1 + (g + 2) // GROUPS)) * 80)
                    for m in range(NB):
                        for k in range(m * GROUP, (m + 1) * GROUP):
                            scoresT(G, g, par, k)
                            if ahead:
                                scores(G + 2, g2, par if g < 2 else 1 - par, k)
                        if m > 0:
                            values(G, g, par, m - 1)
                        elif not at_start(b, g):
                            values(G - 1, (g - 1) % GROUPS, par if g else 1 - par, NB - 1)
                        if m == 0 and not at_end(b, g):
                            turn_maxima(use_m(b, g), G + 1, (g + 1) % 2)
                        if m == 1 and not at_start(b, g):
                            turn_output(use_t(b, g), G - 1)
                        if m == 2 and g == 0 and has_next(b):
                            prep("vt", b + 1)
                        if m >= 2 and g and prepares(b):
                            kind = {(1, 2): "xn", (1, 3): "xa", (2, 2): "q", (2, 3): "k", (3, 2): "v"}.get((g, m))
                            if kind:
                                prep(kind, b + 2)

            batches(pe, body)
            values(G_ALL - 1, GROUPS - 1, (B - 1) % 2, NB - 1)
            turn_output(misc_before(B - 1, GROUPS - 1) + 1, G_ALL - 1)

        @block.scalar
        def _(act):
            act.wait_ge(params_loaded, 16 * PARAM_DMAS)
            act.wait_ge(consts_ready, 3)

            def empty(kind, n):
                use = use_of(kind, n)
                act.wait_ge(misc_filled, use + 1)
                first = isinstance(n, int) and n == 0
                if kind == "xn":
                    if not first:
                        act.wait_ge(xnT_stored, n * 16)
                    op = act.activation(xnT[:, :], ps_misc[:, :], ACT.Copy)
                elif kind == "xa":
                    if not first:
                        act.wait_ge(xa_lo_ready, n)
                    op = act.activation(xaT[:, :], ps_misc[:, :], ACT.Identity, bias=vec[:, 1:2], scale=vec[:, 0:1])
                elif kind == "q":
                    if not first:
                        act.wait_ge(lo_terms, n * 2 - 1)
                    op = act.activation(qT[:, :], ps_misc[:, :], ACT.Identity, bias=bq_scaled[:, :], scale=SCALE)
                elif kind == "k":
                    if not first:
                        act.wait_ge(lo_terms, n * 2)
                    op = act.activation(kT[:, :], ps_misc[:, :], ACT.Identity, bias=vec[:, 3:4])
                else:
                    op = act.activation(vT[:, :], ps_misc[:, :], ACT.Identity, bias=vec[:, 4:5])
                op.then_inc(misc_emptied, 1)

            def place_values(n, par):
                act.wait_ge(misc_filled, use_of("vt", n) + 1)
                act.activation(v_one[:, par, :, :, 0:DH], ps_misc[:, :].rearrange("p (n h d) -> p n h d", n=NB, d=DH),
                               ACT.Copy).then_inc(misc_emptied, 1)

            def read_output(G):
                act.wait_ge(pv_done, G * NB + NB)
                if not (isinstance(G, int) and G == 0):
                    act.wait_ge(recip_ready, G)
                act.activation(oT[:, :], ps_out[:, :], ACT.Copy).then_inc(oT_ready, 1)

            for n in range(2):
                for kind in ("xn", "xa", "q", "k", "v"):
                    empty(kind, n)
                if n == 0:
                    place_values(0, 0)

            def body(b, par):
                for g in range(GROUPS):
                    G = b * GROUPS + g
                    for k in range(GROUP * NB):
                        m, j = k // GROUP, k % GROUP
                        act.wait_ge(scoresT_ready, G * 16 + (k + 1))
                        if j == 0 and not (isinstance(b, int) and G * NB + m < PROBS_RING):
                            act.wait_ge(pv_done, G * NB + (m + 1 - PROBS_RING))
                        act.activation(probs[:, m, j, :], ps_scoresT[:, bank(g, par, k)[0], :], ACT.Exp).then_inc(probs_ready, 1)
                        if k == 5 and not at_start(b, g):
                            read_output(G - 1)
                        if g == 0 and k == 13 and has_next(b):
                            place_values(b + 1, 1 - par)
                        if prepares(b):
                            kind = {(1, 13): "xn", (2, 1): "xa", (2, 9): "q", (3, 1): "k", (3, 13): "v"}.get((g, k))
                            if kind:
                                empty(kind, b + 2)

            batches(act, body)
            read_output(G_ALL - 1)

        @block.vector
        def _(dve):
            dve.memset(v_one[:, :, :, :, DH:DH + 1], 1.0)
            dve.memset(ps_out[:, :], 0.0).then_inc(consts_ready, 1)
            dve.wait_ge(params_loaded, 16 * PARAM_DMAS)
            dve.tensor_copy(wp_hi[:, :, :], wp_raw[:, :, :]).then_inc(consts_ready, 1)
            dve.wait_ge(consts_ready, 2)
            dve.tensor_scalar(bq_scaled[:, :], vec[:, 2:3], SCALE, None, ALU.mult)
            dve.tensor_tensor(wp_lo[:, :, :], wp_raw[:, :, :], wp_hi[:, :, :].bitcast(F32),
                              ALU.subtract).then_inc(consts_ready, 1)

            def statistics(n, par):
                dve.wait_ge(x_loaded[par], (half(n, par) + 1) * 16)
                if not (isinstance(n, int) and n == 0):
                    dve.wait_ge(moments_ready, n * NB)
                for t in range(NB):
                    dve.bn_stats(bn[:, t, :], x_in[:, par, t, :]).then_inc(bn_done, 1)

            def wait_for_statistics(n):
                dve.wait_ge(bn_done, n * NB + NB)
                if not (isinstance(n, int) and n == 0):
                    dve.wait_ge(coef_step, n * COEFS)

            def aggregate():
                for t in range(NB):
                    dve.bn_aggr(moments[:, t, :], bn[:, t, :]).then_inc(moments_ready, 1)

            def round_xa(n):
                dve.wait_ge(misc_emptied, use_of("xa", n) + 1)
                if not (isinstance(n, int) and n == 0):
                    dve.wait_ge(misc_filled, use_of("v", n - 1) + 1)
                dve.tensor_copy(xaT_hi[:, :], xaT[:, :]).then_inc(xa_hi_ready, 1)

            def round_terms(kind, n, par):
                dve.wait_ge(misc_emptied, use_of(kind, n) + 1)
                src = {"q": qT, "k": kT}[kind]
                if kind == "q":
                    dst = q_terms[:, par, HI_SLOTS_Q[0]:HI_SLOTS_Q[1] + 1, :]
                else:
                    dst = k_terms[:, par, HI_SLOTS_K[0]:HI_SLOTS_K[1] + 1:2, :]
                twice = src[:, :].rearrange("p (o t) -> p o t", o=1).broadcast_to([P, 2, T])
                dve.tensor_copy(dst, twice).then_inc(hi_terms, 1)

            def take_maxima(G, g, par, k):
                dve.wait_ge(scores_ready, G * 16 + (k + 1))
                dve.tensor_reduce(maxima[:, g % 2, k:k + 1], ps_scores[:, bank(g, par, k)[0], :], AX_X,
                                  ALU.max).then_inc(maxima_ready, 1)

            def make_shift(use, par):
                dve.wait_ge(misc_filled, use + 1)
                dve.tensor_scalar(shift[:, par, :], ps_misc[0:GROUP * NB, 0:P], -1.0, None,
                                  ALU.mult).then_inc(misc_emptied, 1)

            def finish_output(use, G, g, par):
                dve.wait_ge(misc_filled, use + 1)
                dve.wait_ge(misc_emptied, use)
                if g == 0 and not (isinstance(G, int) and G < 2 * GROUPS):
                    dve.wait_ge(attn_stored, (G // GROUPS - 1) * 16 if isinstance(G, int) else (G - GROUPS) * 4)
                o = ps_misc[:, :].rearrange("p (n j r) -> p n j r", n=NB, r=ROWS)
                dve.reciprocal(recip[:, :, :], o[:, :, :, DH]).then_inc(recip_ready, 1)
                dve.wait_ge(recip_ready, G + 1)
                dst = attn[:, par, :, g * GROUP * DH:(g + 1) * GROUP * DH].rearrange("p n (j d) -> p n j d", d=DH)
                rb = recip[:, :, :].rearrange("p n (j o) -> p n j o", o=1).broadcast_to([P, NB, GROUP, DH])
                dve.tensor_tensor(dst, o[:, :, :, 0:DH], rb, ALU.mult).then_inc(misc_emptied, 1)

            for n in range(2):
                statistics(n, n)
                wait_for_statistics(n)
                aggregate()
                round_xa(n)
                round_terms("q", n, n)
                round_terms("k", n, n)
            for G in range(2):
                for k in range(GROUP * NB):
                    take_maxima(G, G, 0, k)
            make_shift(LEAD_USES - 1, 0)

            def body(b, par):
                for g in range(GROUPS):
                    G = b * GROUPS + g
                    ahead = not isinstance(b, int) or G + 2 < G_ALL
                    for k in range(GROUP * NB):
                        if g == 0 and k == 8 and prepares(b):
                            wait_for_statistics(b + 2)
                        if ahead:
                            take_maxima(G + 2, (g + 2) % GROUPS, par if g < 2 else 1 - par, k)
                        if g == 0 and k == 8 and prepares(b):
                            aggregate()
                        if g == 0 and k == 6 and prepares(b):
                            statistics(b + 2, par)
                        if k == 4 and not at_end(b, g):
                            make_shift(use_m(b, g), (g + 1) % 2)
                        if k == 9 and not at_start(b, g):
                            finish_output(use_t(b, g), G - 1, (g - 1) % GROUPS, par if g else 1 - par)
                        if prepares(b):
                            if (g, k) == (2, 2):
                                round_xa(b + 2)
                            if (g, k) == (2, 14):
                                round_terms("q", b + 2, par)
                            if (g, k) == (3, 4):
                                round_terms("k", b + 2, par)

            batches(dve, body)
            finish_output(misc_before(B - 1, GROUPS - 1) + 1, G_ALL - 1, GROUPS - 1, (B - 1) % 2)


def router_block(nc, env):
    router, router_bias, rank = (env[k] for k in ("router", "router_bias", "rank"))
    B, T, NB, E = (env[k] for k in ("B", "T", "NB", "E"))
    xnT_dram, combine_dram, ident = (env[k] for k in ("xnT_dram", "combine_dram", "ident"))
    TB = B * NB
    RING = 4

    with ExitStack() as ctx:
        def sb(name, shape, dt):
            return ctx.enter_context(nc.sbuf_tensor(name, shape, dt))

        def sem(name):
            return ctx.enter_context(nc.semaphore(name))

        w_router = sb("w_router", [P, E], F32)
        bias8 = sb("bias8", [P, E], F32)
        rank8 = sb("rank8", [P, E], F32)
        xt = sb("r_xt", [P, RING, T], F32)
        big = [sb(f"r_big{n}", [P, TB, E], F32) for n in range(11)]
        one = [sb(f"r_one{n}", [P, TB], F32) for n in range(9)]
        cwT = sb("cwT", [P, T], F32)
        ps_logits = ctx.enter_context(nc.psum_tensor("ps_logits", [P, TB, E], F32))
        ps_cw = ctx.enter_context(nc.psum_tensor("ps_cw", [P, T], F32))
        r_params = sem("r_params")
        xt_loaded = [sem(f"r_xt{n}") for n in range(RING)]
        logits_of = sem("logits_of")
        step = sem("r_step")
        exp_ready = sem("r_exp")
        cw_turned = sem("cw_turned")
        cwT_ready = sem("cwT_ready")
        cw_stored = sem("cw_stored")
        block = ctx.enter_context(nc.Block())

        STEP_DIFF = 12
        STEP_CW = 17

        @block.sync
        def _(sp):
            sp.dma_start(w_router[:, :], router).then_inc(r_params, 16)
            sp.dma_start(bias8[:, :], router_bias.partition_broadcast(P)).then_inc(r_params, 16)
            sp.dma_start(rank8[:, :], rank.partition_broadcast(P)).then_inc(r_params, 16)
            for n in range(B):
                if n >= RING:
                    sp.wait_ge(logits_of, n - RING + 1)
                sp.dma_start(xt[:, n % RING, :], xnT_dram[n]).then_inc(xt_loaded[n % RING], 16)
            sp.wait_ge(cwT_ready, 1)
            sp.dma_start(combine_dram.rearrange("(q p) t -> p q t", p=P),
                         cwT[:, :].rearrange("p (q t) -> p q t", t=P)).then_inc(cw_stored, 16)
            sp.wait_ge(cw_stored, 16)

        @block.tensor
        def _(pe):
            pe.wait_ge(r_params, 48)
            for n in range(B):
                pe.wait_ge(xt_loaded[n % RING], 16 * (n // RING + 1))
                for t in range(NB):
                    mm = pe.matmul(ps_logits[:, n * NB + t, :], xt[:, n % RING, t * P:(t + 1) * P],
                                   w_router[:, :], start=True, stop=True)
                mm.then_inc(logits_of, 1)
            pe.wait_ge(step, STEP_CW)
            cw = big[10][:, :, :].rearrange("p (q b) e -> p q (b e)", q=TB * E // P)
            for q in range(TB * E // P):
                mm = pe.transpose(ps_cw[:, q * P:(q + 1) * P], cw[:, q, :], ident[:, :])
            mm.then_inc(cw_turned, 1)

        @block.scalar
        def _(act):
            act.wait_ge(step, STEP_DIFF)
            act.activation(one[5][:, :], one[4][:, :], ACT.Exp).then_inc(exp_ready, 1)

        @block.vector
        def _(dve):
            def wide(v):
                return v[:, :].rearrange("p (t o) -> p t o", o=1).broadcast_to([P, TB, E])

            def row(v):
                return v[:, :].rearrange("p (o e) -> p o e", o=1).broadcast_to([P, TB, E])

            logits, eq1, key1, sel1, rest, eq2, key2, sel2, part1, part2, cw = (v[:, :, :] for v in big)
            m1, k1, m2, k2, diff, e, total, w1, w2 = one
            dve.wait_ge(r_params, 48)
            dve.wait_ge(logits_of, B)
            steps = (
                lambda: dve.tensor_tensor(logits, ps_logits[:, :, :], row(bias8), ALU.add),
                lambda: dve.tensor_reduce(m1[:, :], logits, AX_X, ALU.max),
                lambda: dve.tensor_tensor(eq1, logits, wide(m1), ALU.is_equal),
                lambda: dve.tensor_tensor(key1, eq1, row(rank8), ALU.mult),
                lambda: dve.tensor_reduce(k1[:, :], key1, AX_X, ALU.max),
                lambda: dve.tensor_tensor(sel1, key1, wide(k1), ALU.is_equal),
                lambda: dve.scalar_tensor_tensor(out=rest, in0=sel1, scalar=FAR_BELOW, in1=logits,
                                                 op0=ALU.mult, op1=ALU.add),
                lambda: dve.tensor_reduce(m2[:, :], rest, AX_X, ALU.max),
                lambda: dve.tensor_tensor(eq2, rest, wide(m2), ALU.is_equal),
                lambda: dve.tensor_tensor(key2, eq2, row(rank8), ALU.mult),
                lambda: dve.tensor_reduce(k2[:, :], key2, AX_X, ALU.max),
                lambda: dve.tensor_tensor(diff[:, :], m2[:, :], m1[:, :], ALU.subtract),
                lambda: dve.tensor_tensor(sel2, key2, wide(k2), ALU.is_equal),
                lambda: dve.tensor_scalar(total[:, :], e[:, :], 1.0, None, ALU.add),
                lambda: dve.reciprocal(w1[:, :], total[:, :]),
                lambda: dve.tensor_tensor(w2[:, :], e[:, :], w1[:, :], ALU.mult),
            )
            assert len(steps) == STEP_CW - 1
            for n, do in enumerate(steps):
                if n == STEP_DIFF + 1:
                    dve.wait_ge(exp_ready, 1)
                do().then_inc(step, 1)
                dve.wait_ge(step, n + 1)
            dve.tensor_tensor(part1, sel1, wide(w1), ALU.mult)
            dve.tensor_tensor(part2, sel2, wide(w2), ALU.mult).then_inc(exp_ready, 1)
            dve.wait_ge(exp_ready, 2)
            dve.tensor_tensor(cw, part1, part2, ALU.add).then_inc(step, 1)
            dve.wait_ge(cw_turned, 1)
            dve.tensor_copy(cwT[:, :], ps_cw[:, :]).then_inc(cwT_ready, 1)


def experts_block(nc, env):
    x, out = env["x"], env["out"]
    B, T, D, NB, NE, E, HID, HC = (env[k] for k in ("B", "T", "D", "NB", "NE", "E", "HID", "HC"))
    xnT_dram, attn_dram, combine_dram, ident, w_hi, w_lo = (
        env[k] for k in ("xnT_dram", "attn_dram", "combine_dram", "ident", "w_hi", "w_lo"))
    U = NE * HC
    UR = E * HC
    RING = 5
    LAG = 4
    SPLIT = 2
    assert U % RING == 0

    with ExitStack() as ctx:
        def sb(name, shape, dt):
            return ctx.enter_context(nc.sbuf_tensor(name, shape, dt))

        def sem(name):
            return ctx.enter_context(nc.semaphore(name))

        xt = sb("e_xt", [P, 2, T], F32)
        x_hi = sb("x_hi", [P, 2, T], F32R)
        x_lo = sb("x_lo", [P, 2, T], F32R)
        cw = sb("cw", [P, 2, NB, E, P], F32)
        gate = sb("gate", [P, RING, T], F32)
        prod = sb("prod", [P, RING, T], F32)
        p_hi = sb("p_hi", [P, RING, T], F32R)
        p_lo = sb("p_lo", [P, RING, T], F32R)
        x_res = sb("x_res", [P, 2, NB, D], F32)
        a_res = sb("a_res", [P, 2, NB, D], F32)
        res = sb("res", [P, 2, NB, D], F32)
        yT = sb("yT", [P, T], F32)
        y_out = sb("y_out", [P, 2, NB, D], F32)
        ps_h1 = ctx.enter_context(nc.psum_tensor("ps_h1", [P, 2, T], F32))
        ps_h3 = ctx.enter_context(nc.psum_tensor("ps_h3", [P, 3, T], F32))
        ps_y = ctx.enter_context(nc.psum_tensor("ps_y", [P, 2, T], F32))
        ps_yt = ctx.enter_context(nc.psum_tensor("ps_yt", [P, T], F32))

        xt_loaded = [sem("e_xt_loaded0"), sem("e_xt_loaded1")]
        cw_loaded = [sem("cw_loaded0"), sem("cw_loaded1")]
        res_loaded = [sem("res_loaded0"), sem("res_loaded1")]
        x_hi_ready = sem("x_hi_ready")
        x_lo_ready = sem("x_lo_ready")
        h1_ready = sem("h1_ready")
        h3_ready = sem("h3_ready")
        gate_ready = sem("gate_ready")
        weighted = sem("weighted")
        prod_ready = sem("prod_ready")
        p_hi_ready = sem("p_hi_ready")
        p_lo_ready = sem("p_lo_ready")
        down_done = sem("down_done")
        res_ready = sem("res_ready")
        yT_ready = sem("yT_ready")
        yt_ready = sem("y_turned")
        y_ready = sem("y_ready")
        y_stored = [sem("y_stored0"), sem("y_stored1")]
        block = ctx.enter_context(nc.Block())

        def batches(eng, body):
            body(0, 0)
            body(1, 1)
            with eng.Fori(1, B // 2 - 1) as pair:
                body(pair * 2, 0)
                body(pair * 2 + 1, 1)
            body(B - 2, 0)
            body(B - 1, 1)

        def is_first(b):
            return isinstance(b, int) and b == 0

        def early(b):
            return isinstance(b, int) and b < 2

        def has_next(b):
            return not isinstance(b, int) or b < B - 1

        def half(b, par):
            return b // 2 if isinstance(b, int) else (b - par) // 2

        def pick(ap, b, names):
            if isinstance(b, int):
                return ap[b]
            return ap[bass.ds(b, 1)].rearrange(f"o {names} -> (o {names[0]}) {names[1:]}")

        @block.sync
        def _(sp):
            cw_rows = NB * E

            def load_x(n, par):
                if not early(n):
                    sp.wait_ge(x_lo_ready, n - 1)
                sp.dma_start(xt[:, par, :], pick(xnT_dram, n, "p t")).then_inc(xt_loaded[par], 16)

            def load_rest(n, par):
                if not early(n):
                    sp.wait_ge(weighted, (n - 1) * UR)
                    sp.wait_ge(res_ready, n - 1)
                src = combine_dram[bass.ds(n * cw_rows, cw_rows)].rearrange("r t -> (r t)")
                sp.dma_start(cw[:, par].rearrange("p n e t -> p (n e t)"),
                             src.partition_broadcast(P)).then_inc(cw_loaded[par], 16)
                src = x[n] if isinstance(n, int) else x[bass.ds(n, 1)].rearrange("o t d -> (o t) d")
                sp.dma_start(x_res[:, par], src.rearrange("(n p) d -> p n d", p=P)).then_inc(res_loaded[par], 16)
                src = attn_dram[n] if isinstance(n, int) else attn_dram[bass.ds(n, 1)].rearrange("o p n d -> (o p) n d")
                sp.dma_start(a_res[:, par], src).then_inc(res_loaded[par], 16)

            def store(n, par):
                sp.wait_ge(y_ready, n + 1)
                dst = out[n] if isinstance(n, int) else out[bass.ds(n, 1)].rearrange("o t d -> (o t) d")
                sp.dma_start(dst.rearrange("(n p) d -> p n d", p=P), y_out[:, par]).then_inc(y_stored[par], 16)

            load_x(0, 0)
            load_rest(0, 0)

            def body(b, par):
                if has_next(b):
                    load_x(b + 1, 1 - par)
                    load_rest(b + 1, 1 - par)
                if not is_first(b):
                    store(b - 1, 1 - par)

            batches(sp, body)
            store(B - 1, (B - 1) % 2)
            for stored in y_stored:
                sp.wait_ge(stored, 8 * B)

        @block.tensor
        def _(pe):
            def up(b, par, u):
                e, hc = u // HC, u % HC
                N = b * U + u
                if not (is_first(b) and u < 2):
                    pe.wait_ge(gate_ready, N - 1)
                for third, ps, ready in ((0, ps_h1[:, u % 2, :], h1_ready), (1, ps_h3[:, u % 3, :], h3_ready)):
                    if third == 1 and not (is_first(b) and u < 3):
                        back = 3 if u >= 3 else {n: u + U - max(v for v in range(U) if v % 3 == n) for n in range(3)}[u]
                        pe.wait_ge(prod_ready, N - (back - 1))
                    cols = slice(third * HID + hc * P, third * HID + (hc + 1) * P)
                    pe.matmul(ps, w_hi[:, e, cols], x_hi[:, par, :], start=True, stop=False)
                    pe.matmul(ps, w_hi[:, e, cols], x_lo[:, par, :], start=False, stop=False)
                    pe.matmul(ps, w_lo[:, e, cols], x_hi[:, par, :], start=False, stop=True).then_inc(ready, 1)

            def down(b, par, u):
                e, hc = u // HC, u % HC
                pe.wait_ge(p_lo_ready, b * U + (u + 1))
                if u == 0 and not early(b):
                    pe.wait_ge(yT_ready, b - 1)
                cols = slice(2 * HID + hc * P, 2 * HID + (hc + 1) * P)
                ps, r = ps_y[:, par, :], u % RING
                pe.matmul(ps, w_hi[:, e, cols], p_hi[:, r, :], start=(u == 0), stop=False)
                pe.matmul(ps, w_hi[:, e, cols], p_lo[:, r, :], start=False, stop=False)
                pe.matmul(ps, w_lo[:, e, cols], p_hi[:, r, :], start=False, stop=(u == U - 1)).then_inc(down_done, 1)

            def turn(b):
                pe.wait_ge(yT_ready, b + 1)
                if not is_first(b):
                    pe.wait_ge(y_ready, b)
                for t in range(NB):
                    mm = pe.transpose(ps_yt[:, t * P:(t + 1) * P], yT[:, t * P:(t + 1) * P], ident[:, :])
                mm.then_inc(yt_ready, 1)

            def body(b, par):
                pe.wait_ge(x_lo_ready, b + 1)
                for u in range(U):
                    up(b, par, u)
                    if u >= LAG:
                        down(b, par, u - LAG)
                    elif not is_first(b):
                        down(b - 1, 1 - par, U + u - LAG)
                    if u == 6 and not is_first(b):
                        turn(b - 1)

            batches(pe, body)
            for u in range(U - LAG, U):
                down(B - 1, (B - 1) % 2, u)
            turn(B - 1)

        @block.scalar
        def _(act):
            def silu(b, u):
                N = b * U + u
                act.wait_ge(h1_ready, N + 1)
                if not (is_first(b) and u < RING):
                    act.wait_ge(prod_ready, N - (RING - 1))
                act.activation(gate[:, u % RING, :], ps_h1[:, u % 2, :], ACT.Silu).then_inc(gate_ready, 1)

            def round_product(b, u):
                N = b * U + u
                if u < UR:
                    act.wait_ge(weighted, b * UR + (u + 1))
                else:
                    act.wait_ge(prod_ready, N + 1)
                if not (is_first(b) and u < RING):
                    act.wait_ge(down_done, N - (RING - 1))
                act.activation(p_hi[:, u % RING, :], prod[:, u % RING, :], ACT.Copy).then_inc(p_hi_ready, 1)

            def read_y(b, par):
                act.wait_ge(down_done, b * U + U)
                if not is_first(b):
                    act.wait_ge(yt_ready, b)
                act.activation(yT[:, :], ps_y[:, par, :], ACT.Copy).then_inc(yT_ready, 1)

            def body(b, par):
                for u in range(U):
                    silu(b, u)
                    if u >= SPLIT:
                        round_product(b, u - SPLIT)
                    elif not is_first(b):
                        round_product(b - 1, U + u - SPLIT)
                    if u == 4 and not is_first(b):
                        read_y(b - 1, 1 - par)

            batches(act, body)
            for u in range(U - SPLIT, U):
                round_product(B - 1, u)
            read_y(B - 1, (B - 1) % 2)

        @block.gpsimd
        def _(pool):
            def body(b, par):
                pool.wait_ge(cw_loaded[par], (half(b, par) + 1) * 16)
                for u in range(UR):
                    e = u // HC
                    pool.wait_ge(prod_ready, b * U + (u + 1))
                    g = prod[:, u % RING, :].rearrange("p (n t) -> p n t", t=P)
                    pool.tensor_tensor(g, g, cw[:, par, :, e, :], ALU.mult).then_inc(weighted, 1)
                    if u == 6:
                        pool.wait_ge(res_loaded[par], (half(b, par) + 1) * 32)
                        if not early(b):
                            pool.wait_ge(y_ready, b - 1)
                        pool.tensor_tensor(res[:, par], x_res[:, par], a_res[:, par], ALU.add).then_inc(res_ready, 1)

            batches(pool, body)

        @block.vector
        def _(dve):
            def split_x(n, par, part):
                if part == 0:
                    dve.wait_ge(xt_loaded[par], (half(n, par) + 1) * 16)
                    if not early(n):
                        dve.wait_ge(h3_ready, (n - 1) * U)
                    dve.tensor_copy(x_hi[:, par, :], xt[:, par, :]).then_inc(x_hi_ready, 1)
                else:
                    dve.wait_ge(x_hi_ready, n + 1)
                    dve.tensor_tensor(x_lo[:, par, :], xt[:, par, :], x_hi[:, par, :].bitcast(F32),
                                      ALU.subtract).then_inc(x_lo_ready, 1)

            def multiply(b, u):
                N = b * U + u
                dve.wait_ge(gate_ready, N + 1)
                dve.wait_ge(h3_ready, N + 1)
                if not (is_first(b) and u < RING):
                    dve.wait_ge(p_lo_ready, N - (RING - 1))
                dve.tensor_tensor(prod[:, u % RING, :], gate[:, u % RING, :], ps_h3[:, u % 3, :],
                                  ALU.mult).then_inc(prod_ready, 1)

            def split_product(b, u):
                N = b * U + u
                r = u % RING
                dve.wait_ge(p_hi_ready, N + 1)
                if not (is_first(b) and u < RING):
                    dve.wait_ge(down_done, N - (RING - 1))
                dve.tensor_tensor(p_lo[:, r, :], prod[:, r, :], p_hi[:, r, :].bitcast(F32),
                                  ALU.subtract).then_inc(p_lo_ready, 1)

            def add_residual(b, par):
                dve.wait_ge(yt_ready, b + 1)
                dve.wait_ge(res_ready, b + 1)
                if not early(b):
                    dve.wait_ge(y_stored[par], half(b, par) * 16)
                dve.tensor_tensor(y_out[:, par], ps_yt[:, :].rearrange("p (n d) -> p n d", d=D), res[:, par],
                                  ALU.add).then_inc(y_ready, 1)

            split_x(0, 0, 0)
            split_x(0, 0, 1)

            def body(b, par):
                for u in range(U):
                    multiply(b, u)
                    if u >= SPLIT:
                        split_product(b, u - SPLIT)
                    elif not is_first(b):
                        split_product(b - 1, U + u - SPLIT)
                    if u == 7 and not is_first(b):
                        add_residual(b - 1, 1 - par)
                    if u in (10, 12) and has_next(b):
                        split_x(b + 1, 1 - par, (u - 10) // 2)

            batches(dve, body)
            for u in range(U - SPLIT, U):
                split_product(B - 1, u)
            add_residual(B - 1, (B - 1) % 2)


def kernel(**inputs):
    import numpy as np
    import concourse.bacc as bacc
    from concourse.bass_utils import run_bass_kernel_spmd as run

    a = {k.replace("L0_attn_", "a_").replace("L0_ffn_", "f_"): np.asarray(v) for k, v in inputs.items()}
    x = np.ascontiguousarray(a["a_x"])
    D = x.shape[2]

    def first_layer(w):
        return w.transpose(2, 0, 1)

    def second_layer(w):
        n, d, h = w.shape
        return w.reshape(n, d, h // 128, 128).transpose(3, 0, 2, 1).reshape(128, n, h)

    every = {k: np.concatenate([a["f_" + k], a["f_s" + k]]) for k in ("w1", "w3", "w2")}
    laid = {
        "x": x,
        "vecs": np.stack([a[k] for k in ("a_ln_g", "a_ln_b", "a_bq", "a_bk", "a_bv")], 1),
        "wqkv": np.stack([a["a_Wq"], a["a_Wk"], a["a_Wv"]], 1),
        "experts": np.concatenate(
            [first_layer(every["w1"]), first_layer(every["w3"]), second_layer(every["w2"])], 2),
        "router": a["f_router_w"].T,
        "router_bias": a["f_expert_bias"],
        "rank": np.arange(a["f_router_w"].shape[0], 0, -1).astype(np.float32),
        "ident_in": np.eye(D, dtype=np.float32),
    }
    nc = bacc.Bacc("TRN2", target_bir_lowering=False, num_devices=1)
    arrays, args = {}, []
    for name, v in laid.items():
        v = np.ascontiguousarray(v)
        arrays[f"{name}_dram"] = v
        args.append(nc.dram_tensor(f"{name}_dram", v.shape, mybir.dt.from_np(v.dtype), kind="ExternalInput").ap())
    args.append(nc.dram_tensor("out_dram", x.shape, F32, kind="ExternalOutput").ap())
    prenorm_attention_moe(nc, *args)
    r = run(nc, [arrays], core_ids=[0])
    return r.results[0]["out_dram"]
```

```python
from contextlib import ExitStack

import concourse.bass as bass
from concourse import mybir

F32 = mybir.dt.float32
F32R = mybir.dt.float32r
U32 = mybir.dt.uint32
ALU = mybir.AluOpType
ACT = mybir.ActivationFunctionType
AX_X = mybir.AxisListType.X

P = 128
EPS = 1e-5
TERMS = 4
GROUP = 4
HI_SLOTS_Q = (0, 1)
LO_SLOT_Q = 2
HI_SLOTS_K = (0, 2)
LO_SLOT_K = 1
SHIFT_SLOT = 3
PROBS_RING = 4
TOP_K = 2
BANKS = 3
FAR_BELOW = -3.0e38


def prenorm_attention_moe(nc, x, vecs, wqkv, experts, router, router_bias, rank, tile_no, tri, ident_in, out):
    B, T, D = x.shape
    E = router.shape[1]
    NE = experts.shape[1]
    HID = experts.shape[2] // 3
    NB = T // P
    TB = B * NB
    HC = HID // P
    HEADS = 16
    DH = D // HEADS
    GROUPS = HEADS // GROUP
    SCALE = float(DH) ** -0.5
    ROWS = DH * TERMS
    G_ALL = B * GROUPS
    TILES = (TOP_K * B * T + E * (T - 1)) // T
    assert D == P and ROWS * GROUP == P and T == 512 and B % 2 == 0 and GROUPS == 4 and NB == 4
    assert tile_no.shape[0] >= TILES >= B

    def scratch(name, shape):
        return nc.dram_tensor(name, shape, F32, kind="Internal").ap()

    weights_dram = scratch("weights_dram", [NE, P, 2, 3 * HID])
    slots_dram = scratch("slots_dram", [TILES * T, D])
    routed_dram = scratch("routed_dram", [TILES * T, D])
    base_dram = scratch("base_dram", [B, P, NB, D])

    with ExitStack() as outer:
        def keep(name, shape, dt):
            return outer.enter_context(nc.sbuf_tensor(name, shape, dt))

        ident = keep("ident", [P, P], F32)
        xn = keep("xn", [P, TB, D], F32)
        r2 = keep("r2", [P, TB], F32)
        picks = [keep(f"pick{k}", [P, TB], F32) for k in range(TOP_K)]
        slots = [keep(f"slot{k}", [P, TB], U32) for k in range(TOP_K)]
        tile_expert = keep("tile_expert", [P, TILES], U32)
        env = locals()
        route_block(nc, env)
        shared_block(nc, env)
        routed_block(nc, env)
        attention_block(nc, env)


def attention_block(nc, env):
    vecs, wqkv, out = (env[k] for k in ("vecs", "wqkv", "out"))
    B, T, D, NB, NE, HID, DH, HEADS, GROUPS, ROWS, G_ALL, SCALE = (
        env[k] for k in ("B", "T", "D", "NB", "NE", "HID", "DH", "HEADS", "GROUPS", "ROWS", "G_ALL", "SCALE"))
    routed_dram, base_dram, ident, xn_all, r2_all, picks, slots = (
        env[k] for k in ("routed_dram", "base_dram", "ident", "xn", "r2", "picks", "slots"))
    LAST_PREP = B - 2

    with ExitStack() as ctx:
        def sb(name, shape, dt):
            return ctx.enter_context(nc.sbuf_tensor(name, shape, dt))

        def sem(name):
            return ctx.enter_context(nc.semaphore(name))

        vec = sb("vec", [P, 5], F32)
        bq_scaled = sb("bq_scaled", [P, 1], F32)
        wp_raw = sb("wp_raw", [P, 3, D], F32)
        wp_hi = sb("wp_hi", [P, 3, D], F32R)
        wp_lo = sb("wp_lo", [P, 3, D], F32R)
        xn = sb("xn_tile", [P, 2, NB, D], F32)
        xa = sb("xa", [P, NB, D], F32)
        r2 = sb("r2_tile", [P, NB], F32)
        slot = sb("slot_tile", [P, TOP_K, NB], U32)
        pick = sb("pick_tile", [P, TOP_K, NB], F32)
        routed = sb("routed", [P, TOP_K, NB, D], F32)
        base = sb("base", [P, 2, NB, D], F32)
        total = sb("total", [P, 2, NB, D], F32)
        xaT = sb("xaT", [P, T], F32)
        xaT_hi = sb("xaT_hi", [P, T], F32R)
        xaT_lo = sb("xaT_lo", [P, T], F32R)
        qT = sb("qT", [P, T], F32)
        kT = sb("kT", [P, T], F32)
        vT = sb("vT", [P, T], F32)
        q_terms = sb("q_terms", [P, 2, TERMS, T], F32R)
        k_terms = sb("k_terms", [P, 2, TERMS, T], F32R)
        q_stack = sb("q_stack", [P, GROUPS, GROUP, T], F32R)
        k_stack = sb("k_stack", [P, GROUPS, T], F32R)
        v_one = sb("v_one", [P, 2, NB, HEADS, DH + 1], F32)
        maxima = sb("maxima", [P, 2, GROUP * NB], F32)
        shift = sb("shift", [GROUP * NB, 2, P], F32R)
        probs = sb("probs", [P, PROBS_RING, GROUP, T], F32)
        oT = sb("oT", [P, T], F32)
        recip = sb("recip", [P, NB, GROUP], F32)
        fence = sb("fence", [P, 1], F32)
        attn = sb("attn", [P, 2, NB, D], F32)

        ps_scores = ctx.enter_context(nc.psum_tensor("ps_scores", [P, BANKS, T], F32))
        ps_scoresT = ctx.enter_context(nc.psum_tensor("ps_scoresT", [P, BANKS, T], F32))
        ps_out = ctx.enter_context(nc.psum_tensor("ps_out", [P, T], F32))
        ps_misc = ctx.enter_context(nc.psum_tensor("ps_misc", [P, T], F32))

        params_loaded = sem("params_loaded")
        consts_ready = sem("consts_ready")
        pool_consts = sem("pool_consts")
        xn_loaded = [sem("xn_loaded0"), sem("xn_loaded1")]
        r2_taken = sem("r2_taken")
        xa_ready = sem("xa_ready")
        picked = sem("picked")
        gathered = [sem("gathered0"), sem("gathered1")]
        base_loaded = [sem("base_loaded0"), sem("base_loaded1")]
        total_step = sem("total_step")
        total_stored = [sem("total_stored0"), sem("total_stored1")]
        misc_filled = sem("misc_filled")
        misc_emptied = sem("misc_emptied")
        xa_hi_ready = sem("xa_hi_ready")
        xa_lo_ready = sem("xa_lo_ready")
        hi_terms = sem("hi_terms")
        lo_terms = sem("lo_terms")
        stacks_loaded = [sem(f"stacks_loaded{g}") for g in range(GROUPS)]
        scores_ready = sem("scores_ready")
        maxima_ready = sem("maxima_ready")
        shift_loaded = sem("shift_loaded")
        scoresT_ready = sem("scoresT_ready")
        probs_ready = sem("probs_ready")
        pv_done = sem("pv_done")
        oT_ready = sem("oT_ready")
        recip_ready = sem("recip_ready")

        PARAM_DMAS = 2
        TOTAL = TOP_K + 3
        USES = 2 * GROUPS + 5
        block = ctx.enter_context(nc.Block())

        LEAD_USES = 10
        PREP_BEFORE = (0, 1, 2, 4)

        def misc_before(b, g):
            if not isinstance(b, int):
                return b * USES + (LEAD_USES + 2 * g - 1 + PREP_BEFORE[g])
            G = b * GROUPS + g
            prep = 5 * min(b, LAST_PREP)
            if b < LAST_PREP:
                prep += PREP_BEFORE[g]
            elif b == LAST_PREP:
                prep += 1 if g else 0
            else:
                prep += 1
            return LEAD_USES + max(G - 1, 0) + min(G, G_ALL - 1) + prep

        def use_m(b, g):
            return misc_before(b, g)

        def use_t(b, g):
            last = isinstance(b, int) and b == B - 1 and g == GROUPS - 1
            return misc_before(b, g) + (0 if last else 1)

        def use_prep(b, g, n):
            first = isinstance(b, int) and b == 0 and g == 0
            return misc_before(b, g) + (1 if first else 2) + n

        def use_of(kind, n):
            lead = {"xa": 0, "q": 1, "k": 2, "v": 3, "vt": 4}[kind]
            if isinstance(n, int) and n == 0:
                return lead
            if kind == "vt":
                return use_prep(n - 1, 0, 0)
            if isinstance(n, int) and n == 1:
                return 5 + lead
            g, k = {"xa": (1, 0), "q": (2, 0), "k": (2, 1), "v": (3, 0)}[kind]
            return use_prep(n - 2, g, k)

        def bank(g, par, k):
            ring = 2 * GROUPS * GROUP * NB
            at = (par * GROUPS + g) * GROUP * NB + k
            if at >= BANKS:
                return at % BANKS, BANKS
            last = max(v for v in range(ring) if v % BANKS == at)
            return at, at + ring - last

        def batches(eng, body):
            body(0, 0)
            body(1, 1)
            with eng.Fori(1, B // 2 - 1) as pair:
                body(pair * 2, 0)
                body(pair * 2 + 1, 1)
            body(B - 2, 0)
            body(B - 1, 1)

        def at_start(b, g=0):
            return isinstance(b, int) and b == 0 and g == 0

        def at_end(b, g=3):
            return isinstance(b, int) and b == B - 1 and g == GROUPS - 1

        def prepares(b):
            return not isinstance(b, int) or b < LAST_PREP

        def has_next(b):
            return not isinstance(b, int) or b < B - 1

        def half(b, par):
            return b // 2 if isinstance(b, int) else (b - par) // 2

        @block.sync
        def _(sp):
            sp.dma_start(vec[:, :], vecs).then_inc(params_loaded, 16)
            sp.dma_start(wp_raw[:, :, :], wqkv).then_inc(params_loaded, 16)

            def load_xn(n, par):
                if not (isinstance(n, int) and n < 2):
                    sp.wait_ge(xa_ready, n - 1)
                src = xn_all[:, bass.ds(n * NB, NB), :]
                sp.dma_start(xn[:, par], src).then_inc(xn_loaded[par], 16)

            def load_base(n, par):
                if not (isinstance(n, int) and n < 2):
                    sp.wait_ge(total_step, (n - 1) * TOTAL)
                src = base_dram[n] if isinstance(n, int) else base_dram[bass.ds(n, 1)].rearrange("o p n d -> (o p) n d")
                sp.dma_start(base[:, par], src).then_inc(base_loaded[par], 16)

            def store_total(n, par):
                sp.wait_ge(total_step, n * TOTAL + TOTAL)
                dst = out[n] if isinstance(n, int) else out[bass.ds(n, 1)].rearrange("o t d -> (o t) d")
                sp.dma_start(dst.rearrange("(n p) d -> p n d", p=P), total[:, par]).then_inc(total_stored[par], 16)

            def load_stacks(n, par, g, freed):
                sp.wait_ge(lo_terms, n * 2 + 2)
                if freed is not None:
                    sp.wait_ge(scoresT_ready, freed)
                rows = GROUP * DH
                sp.dma_start(k_stack[:, g, :].bitcast(F32),
                             k_terms[g * rows:(g + 1) * rows, par].bitcast(F32)).then_inc(stacks_loaded[g], 16)
                for j in range(GROUP):
                    h = g * GROUP + j
                    sp.dma_start(q_stack[j * ROWS:(j + 1) * ROWS, g, j, :].bitcast(F32),
                                 q_terms[h * DH:(h + 1) * DH, par].bitcast(F32)).then_inc(stacks_loaded[g], 16)

            def load_shift(g, par, emptied):
                sp.wait_ge(misc_emptied, emptied)
                for j in range(GROUP):
                    row = j * ROWS + SHIFT_SLOT
                    sp.dma_start(q_stack[row:row + 1, g, j, :].bitcast(F32),
                                 shift[j * NB:(j + 1) * NB, par, :].bitcast(F32)).then_inc(shift_loaded, 16)

            load_xn(0, 0)
            load_xn(1, 1)
            load_base(0, 0)
            sp.wait_ge(pool_consts, 2)
            for g in range(GROUPS):
                load_stacks(0, 0, g, None)
            load_shift(0, 0, LEAD_USES)

            def body(b, par):
                for g in range(GROUPS):
                    G = b * GROUPS + g
                    if g == 0 and prepares(b):
                        load_xn(b + 2, par)
                    if not at_end(b, g):
                        load_shift((g + 1) % GROUPS, (g + 1) % 2, use_m(b, g) + 1)
                    if g == 1 and has_next(b):
                        load_base(b + 1, 1 - par)
                    if g == 2 and not (isinstance(b, int) and b == 0):
                        store_total(b - 1, 1 - par)
                    if has_next(b):
                        load_stacks(b + 1, 1 - par, g, (G + 1) * (GROUP * NB))

            batches(sp, body)
            store_total(B - 1, (B - 1) % 2)
            for stored in total_stored:
                sp.wait_ge(stored, 8 * B)

        @block.gpsimd
        def _(pool):
            pool.memset(q_stack[:, :, :, :].bitcast(F32), 0.0).then_inc(pool_consts, 1)
            pool.memset(fence[:, :], 0.0)
            pool.memset(q_terms[:, :, SHIFT_SLOT, :].bitcast(F32), 0.0)
            pool.memset(k_terms[:, :, SHIFT_SLOT, :].bitcast(F32), 1.0).then_inc(pool_consts, 1)

            def wide(v):
                return v.rearrange("p (n o) -> p n o", o=1).broadcast_to([P, NB, D])

            def take_r2(n):
                pool.tensor_copy(r2[:, :], r2_all[:, bass.ds(n * NB, NB)]).then_inc(r2_taken, 1)

            def scale_xn(n, par):
                pool.wait_ge(r2_taken, n + 1)
                if not (isinstance(n, int) and n == 0):
                    pool.wait_ge(misc_filled, use_of("xa", n - 1) + 1)
                pool.wait_ge(xn_loaded[par], (half(n, par) + 1) * 16)
                pool.tensor_tensor(xa[:, :, :], xn[:, par], wide(r2[:, :]), ALU.mult).then_inc(xa_ready, 1)

            def take_picks(n):
                for k in range(TOP_K):
                    pool.tensor_copy(slot[:, k, :], slots[k][:, bass.ds(n * NB, NB)]).then_inc(picked, 1)
                    pool.tensor_copy(pick[:, k, :], picks[k][:, bass.ds(n * NB, NB)]).then_inc(picked, 1)

            def gather(n):
                pool.wait_ge(picked, n * (2 * TOP_K) + 2 * TOP_K)
                pool.tensor_tensor(fence[:, :], fence[:, :], fence[:, :], ALU.mult)
                for k in range(TOP_K):
                    for t in range(NB):
                        pool.indirect_dma_start(routed[:, k, t, :], None, routed_dram,
                                                bass.IndirectOffsetOnAxis(ap=slot[:, k, t:t + 1], axis=0)
                                                ).then_inc(gathered[k], 16)

            def add_up(n, par):
                step = n * TOTAL
                for k in range(TOP_K):
                    pool.wait_ge(gathered[k], n * (16 * NB) + 16 * NB)
                    pool.tensor_tensor(routed[:, k], routed[:, k], wide(pick[:, k, :]), ALU.mult).then_inc(total_step, 1)
                pool.wait_ge(base_loaded[par], (half(n, par) + 1) * 16)
                if not (isinstance(n, int) and n < 2):
                    pool.wait_ge(total_stored[par], half(n, par) * 16)
                pool.wait_ge(total_step, step + TOP_K)
                pool.tensor_tensor(total[:, par], routed[:, 0], routed[:, 1], ALU.add).then_inc(total_step, 1)
                pool.wait_ge(total_step, step + (TOP_K + 1))
                pool.tensor_tensor(total[:, par], total[:, par], base[:, par], ALU.add).then_inc(total_step, 1)
                last = misc_before(B - 1, GROUPS - 1) + 2 if isinstance(n, int) and n == B - 1 else use_t(n + 1, 0) + 1
                pool.wait_ge(misc_emptied, last)
                pool.wait_ge(total_step, step + (TOP_K + 2))
                pool.tensor_tensor(total[:, par], total[:, par], attn[:, par], ALU.add).then_inc(total_step, 1)

            def split_xa(n):
                pool.wait_ge(xa_hi_ready, n + 1)
                if not (isinstance(n, int) and n == 0):
                    pool.wait_ge(misc_filled, use_of("v", n - 1) + 1)
                pool.tensor_tensor(xaT_lo[:, :], xaT[:, :], xaT_hi[:, :].bitcast(F32),
                                   ALU.subtract).then_inc(xa_lo_ready, 1)

            def split_qk(n, par):
                pool.wait_ge(hi_terms, n * 2 + 1)
                pool.tensor_tensor(q_terms[:, par, LO_SLOT_Q, :], qT[:, :],
                                   q_terms[:, par, HI_SLOTS_Q[0], :].bitcast(F32), ALU.subtract).then_inc(lo_terms, 1)
                pool.wait_ge(hi_terms, n * 2 + 2)
                pool.tensor_tensor(k_terms[:, par, LO_SLOT_K, :], kT[:, :],
                                   k_terms[:, par, HI_SLOTS_K[0], :].bitcast(F32), ALU.subtract).then_inc(lo_terms, 1)

            for n in range(2):
                take_r2(n)
                scale_xn(n, n)
                split_xa(n)
                if n == 0:
                    pool.wait_ge(pool_consts, 2)
                split_qk(n, n)

            def body(b, par):
                if not (isinstance(b, int) and b == 0):
                    take_picks(b - 1)
                if prepares(b):
                    take_r2(b + 2)
                if not (isinstance(b, int) and b == 0):
                    gather(b - 1)
                if prepares(b):
                    scale_xn(b + 2, par)
                if not (isinstance(b, int) and b == 0):
                    add_up(b - 1, 1 - par)
                if prepares(b):
                    split_xa(b + 2)
                    split_qk(b + 2, par)

            batches(pool, body)
            take_picks(B - 1)
            gather(B - 1)
            add_up(B - 1, (B - 1) % 2)

        @block.tensor
        def _(pe):
            def begin(use):
                if not (isinstance(use, int) and use == 0):
                    pe.wait_ge(misc_emptied, use)

            def turn_blocks(use, src):
                begin(use)
                for t in range(NB):
                    last = pe.transpose(ps_misc[:, t * P:(t + 1) * P], src[:, t, :], ident[:, :])
                last.then_inc(misc_filled, 1)

            def prep(kind, n):
                use = use_of(kind, n)
                if kind == "xa":
                    pe.wait_ge(xa_ready, n + 1)
                    turn_blocks(use, xa)
                elif kind == "vt":
                    pe.wait_ge(misc_emptied, use_of("v", n) + 1)
                    turn_blocks(use, vT[:, :].rearrange("p (n q) -> p n q", q=P))
                else:
                    w = "qkv".index(kind)
                    pe.wait_ge(xa_lo_ready, n + 1)
                    begin(use)
                    pe.matmul(ps_misc[:, :], wp_hi[:, w, :], xaT_hi[:, :], start=True, stop=False)
                    pe.matmul(ps_misc[:, :], wp_hi[:, w, :], xaT_lo[:, :], start=False, stop=False)
                    pe.matmul(ps_misc[:, :], wp_lo[:, w, :], xaT_hi[:, :], start=False,
                              stop=True).then_inc(misc_filled, 1)

            def scores(G, g, par, k):
                j, n = k // NB, k % NB
                at, back = bank(g, par, k)
                if not (isinstance(G, int) and G * 16 + k < BANKS):
                    pe.wait_ge(maxima_ready, G * 16 + (k + 1 - back))
                pe.matmul(ps_scores[:, at, :], q_stack[:, g, j, n * P:(n + 1) * P],
                          k_stack[:, g, :], start=True, stop=True).then_inc(scores_ready, 1)

            def scoresT(G, g, par, k):
                m, j = k // GROUP, k % GROUP
                at, back = bank(g, par, k)
                if not (isinstance(G, int) and G * 16 + k < BANKS):
                    pe.wait_ge(probs_ready, G * 16 + (k + 1 - back))
                pe.matmul(ps_scoresT[:, at, :], k_stack[:, g, m * P:(m + 1) * P],
                          q_stack[:, g, j, :], start=True, stop=True).then_inc(scoresT_ready, 1)

            def values(G, g, par, m):
                pe.wait_ge(probs_ready, G * 16 + (m + 1) * GROUP)
                if m == 0 and not (isinstance(G, int) and G == 0):
                    pe.wait_ge(oT_ready, G)
                for j in range(GROUP):
                    mm = pe.matmul(ps_out[j * ROWS:j * ROWS + DH + 1, :], v_one[:, par, m, g * GROUP + j, :],
                                   probs[:, m, j, :], start=(m == 0), stop=(m == NB - 1),
                                   tile_position=(0, j * ROWS))
                mm.then_inc(pv_done, 1)

            def turn_maxima(use, G, par):
                pe.wait_ge(maxima_ready, G * 16 + 16)
                begin(use)
                pe.transpose(ps_misc[0:GROUP * NB, 0:P], maxima[:, par, :], ident[:, :]).then_inc(misc_filled, 1)

            def turn_output(use, G):
                pe.wait_ge(oT_ready, G + 1)
                turn_blocks(use, oT[:, :].rearrange("p (n q) -> p n q", q=P))

            pe.wait_ge(params_loaded, 16 * PARAM_DMAS)
            pe.wait_ge(consts_ready, 3)
            for kind in ("xa", "q", "k", "v", "vt"):
                prep(kind, 0)
            for kind in ("xa", "q", "k", "v"):
                prep(kind, 1)
            for G in range(2):
                pe.wait_ge(stacks_loaded[G], 80)
                for k in range(GROUP * NB):
                    scores(G, G, 0, k)
            turn_maxima(LEAD_USES - 1, 0, 0)

            def body(b, par):
                for g in range(GROUPS):
                    G = b * GROUPS + g
                    ahead = not isinstance(b, int) or G + 2 < G_ALL
                    pe.wait_ge(shift_loaded, G * (16 * GROUP) + 16 * GROUP)
                    if ahead:
                        g2 = (g + 2) % GROUPS
                        pe.wait_ge(stacks_loaded[g2], (b + (1 + (g + 2) // GROUPS)) * 80)
                    for m in range(NB):
                        for k in range(m * GROUP, (m + 1) * GROUP):
                            scoresT(G, g, par, k)
                            if ahead:
                                scores(G + 2, g2, par if g < 2 else 1 - par, k)
                        if m > 0:
                            values(G, g, par, m - 1)
                        elif not at_start(b, g):
                            values(G - 1, (g - 1) % GROUPS, par if g else 1 - par, NB - 1)
                        if m == 0 and not at_end(b, g):
                            turn_maxima(use_m(b, g), G + 1, (g + 1) % 2)
                        if m == 1 and not at_start(b, g):
                            turn_output(use_t(b, g), G - 1)
                        if m == 2 and g == 0 and has_next(b):
                            prep("vt", b + 1)
                        if m >= 2 and g and prepares(b):
                            kind = {(1, 3): "xa", (2, 2): "q", (2, 3): "k", (3, 2): "v"}.get((g, m))
                            if kind:
                                prep(kind, b + 2)

            batches(pe, body)
            values(G_ALL - 1, GROUPS - 1, (B - 1) % 2, NB - 1)
            turn_output(misc_before(B - 1, GROUPS - 1) + 1, G_ALL - 1)

        @block.scalar
        def _(act):
            act.wait_ge(params_loaded, 16 * PARAM_DMAS)
            act.wait_ge(consts_ready, 3)

            def empty(kind, n):
                use = use_of(kind, n)
                act.wait_ge(misc_filled, use + 1)
                first = isinstance(n, int) and n == 0
                if kind == "xa":
                    if not first:
                        act.wait_ge(xa_lo_ready, n)
                    op = act.activation(xaT[:, :], ps_misc[:, :], ACT.Identity, bias=vec[:, 1:2], scale=vec[:, 0:1])
                elif kind == "q":
                    if not first:
                        act.wait_ge(lo_terms, n * 2 - 1)
                    op = act.activation(qT[:, :], ps_misc[:, :], ACT.Identity, bias=bq_scaled[:, :], scale=SCALE)
                elif kind == "k":
                    if not first:
                        act.wait_ge(lo_terms, n * 2)
                    op = act.activation(kT[:, :], ps_misc[:, :], ACT.Identity, bias=vec[:, 3:4])
                else:
                    op = act.activation(vT[:, :], ps_misc[:, :], ACT.Identity, bias=vec[:, 4:5])
                op.then_inc(misc_emptied, 1)

            def place_values(n, par):
                act.wait_ge(misc_filled, use_of("vt", n) + 1)
                act.activation(v_one[:, par, :, :, 0:DH], ps_misc[:, :].rearrange("p (n h d) -> p n h d", n=NB, d=DH),
                               ACT.Copy).then_inc(misc_emptied, 1)

            def read_output(G):
                act.wait_ge(pv_done, G * NB + NB)
                if not (isinstance(G, int) and G == 0):
                    act.wait_ge(recip_ready, G)
                act.activation(oT[:, :], ps_out[:, :], ACT.Copy).then_inc(oT_ready, 1)

            for n in range(2):
                for kind in ("xa", "q", "k", "v"):
                    empty(kind, n)
                if n == 0:
                    place_values(0, 0)

            def body(b, par):
                for g in range(GROUPS):
                    G = b * GROUPS + g
                    for k in range(GROUP * NB):
                        m, j = k // GROUP, k % GROUP
                        act.wait_ge(scoresT_ready, G * 16 + (k + 1))
                        if j == 0 and not (isinstance(b, int) and G * NB + m < PROBS_RING):
                            act.wait_ge(pv_done, G * NB + (m + 1 - PROBS_RING))
                        act.activation(probs[:, m, j, :], ps_scoresT[:, bank(g, par, k)[0], :], ACT.Exp).then_inc(probs_ready, 1)
                        if k == 5 and not at_start(b, g):
                            read_output(G - 1)
                        if g == 0 and k == 13 and has_next(b):
                            place_values(b + 1, 1 - par)
                        if prepares(b):
                            kind = {(2, 1): "xa", (2, 9): "q", (3, 1): "k", (3, 13): "v"}.get((g, k))
                            if kind:
                                empty(kind, b + 2)

            batches(act, body)
            read_output(G_ALL - 1)

        @block.vector
        def _(dve):
            dve.memset(v_one[:, :, :, :, DH:DH + 1], 1.0)
            dve.memset(ps_out[:, :], 0.0).then_inc(consts_ready, 1)
            dve.wait_ge(params_loaded, 16 * PARAM_DMAS)
            dve.tensor_copy(wp_hi[:, :, :], wp_raw[:, :, :]).then_inc(consts_ready, 1)
            dve.wait_ge(consts_ready, 2)
            dve.tensor_scalar(bq_scaled[:, :], vec[:, 2:3], SCALE, None, ALU.mult)
            dve.tensor_tensor(wp_lo[:, :, :], wp_raw[:, :, :], wp_hi[:, :, :].bitcast(F32),
                              ALU.subtract).then_inc(consts_ready, 1)

            def round_xa(n):
                dve.wait_ge(misc_emptied, use_of("xa", n) + 1)
                if not (isinstance(n, int) and n == 0):
                    dve.wait_ge(misc_filled, use_of("v", n - 1) + 1)
                dve.tensor_copy(xaT_hi[:, :], xaT[:, :]).then_inc(xa_hi_ready, 1)

            def round_terms(kind, n, par):
                dve.wait_ge(misc_emptied, use_of(kind, n) + 1)
                src = {"q": qT, "k": kT}[kind]
                if kind == "q":
                    dst = q_terms[:, par, HI_SLOTS_Q[0]:HI_SLOTS_Q[1] + 1, :]
                else:
                    dst = k_terms[:, par, HI_SLOTS_K[0]:HI_SLOTS_K[1] + 1:2, :]
                twice = src[:, :].rearrange("p (o t) -> p o t", o=1).broadcast_to([P, 2, T])
                dve.tensor_copy(dst, twice).then_inc(hi_terms, 1)

            def take_maxima(G, g, par, k):
                dve.wait_ge(scores_ready, G * 16 + (k + 1))
                dve.tensor_reduce(maxima[:, g % 2, k:k + 1], ps_scores[:, bank(g, par, k)[0], :], AX_X,
                                  ALU.max).then_inc(maxima_ready, 1)

            def make_shift(use, par):
                dve.wait_ge(misc_filled, use + 1)
                dve.tensor_scalar(shift[:, par, :], ps_misc[0:GROUP * NB, 0:P], -1.0, None,
                                  ALU.mult).then_inc(misc_emptied, 1)

            def finish_output(use, G, g, par, b_before=None):
                dve.wait_ge(misc_filled, use + 1)
                dve.wait_ge(misc_emptied, use)
                if g == 0 and not (isinstance(G, int) and G < 2 * GROUPS):
                    added = G // GROUPS - 1 if isinstance(G, int) else b_before
                    dve.wait_ge(total_step, added * TOTAL)
                o = ps_misc[:, :].rearrange("p (n j r) -> p n j r", n=NB, r=ROWS)
                dve.reciprocal(recip[:, :, :], o[:, :, :, DH]).then_inc(recip_ready, 1)
                dve.wait_ge(recip_ready, G + 1)
                dst = attn[:, par, :, g * GROUP * DH:(g + 1) * GROUP * DH].rearrange("p n (j d) -> p n j d", d=DH)
                rb = recip[:, :, :].rearrange("p n (j o) -> p n j o", o=1).broadcast_to([P, NB, GROUP, DH])
                dve.tensor_tensor(dst, o[:, :, :, 0:DH], rb, ALU.mult).then_inc(misc_emptied, 1)

            for n in range(2):
                round_xa(n)
                round_terms("q", n, n)
                round_terms("k", n, n)
            for G in range(2):
                for k in range(GROUP * NB):
                    take_maxima(G, G, 0, k)
            make_shift(LEAD_USES - 1, 0)

            def body(b, par):
                for g in range(GROUPS):
                    G = b * GROUPS + g
                    ahead = not isinstance(b, int) or G + 2 < G_ALL
                    for k in range(GROUP * NB):
                        if ahead:
                            take_maxima(G + 2, (g + 2) % GROUPS, par if g < 2 else 1 - par, k)
                        if k == 4 and not at_end(b, g):
                            make_shift(use_m(b, g), (g + 1) % 2)
                        if k == 9 and not at_start(b, g):
                            finish_output(use_t(b, g), G - 1, (g - 1) % GROUPS, par if g else 1 - par, b - 1)
                        if prepares(b):
                            if (g, k) == (2, 2):
                                round_xa(b + 2)
                            if (g, k) == (2, 14):
                                round_terms("q", b + 2, par)
                            if (g, k) == (3, 4):
                                round_terms("k", b + 2, par)

            batches(dve, body)
            finish_output(misc_before(B - 1, GROUPS - 1) + 1, G_ALL - 1, GROUPS - 1, (B - 1) % 2)


def route_block(nc, env):
    x, experts, router, router_bias, rank, tile_no, tri, ident_in = (
        env[k] for k in ("x", "experts", "router", "router_bias", "rank", "tile_no", "tri", "ident_in"))
    B, T, D, NB, TB, E, NE, HID, TILES = (env[k] for k in ("B", "T", "D", "NB", "TB", "E", "NE", "HID", "TILES"))
    weights_dram, slots_dram, ident, xn, r2, picks, slots, tile_expert = (
        env[k] for k in ("weights_dram", "slots_dram", "ident", "xn", "r2", "picks", "slots", "tile_expert"))
    CHUNK = 4
    CHUNKS = B // CHUNK
    CB = CHUNK * NB

    with ExitStack() as ctx:
        def sb(name, shape, dt=F32):
            return ctx.enter_context(nc.sbuf_tensor(name, shape, dt))

        def sem(name):
            return ctx.enter_context(nc.semaphore(name))

        w_router = sb("w_router", [P, E])
        bias8 = sb("bias8", [P, E])
        rank8 = sb("rank8", [P, E])
        numbers = sb("numbers", [P, TILES])
        before = sb("before", [P, P])
        ones = sb("ones", [P, P])
        zeros = sb("zeros", [P, NB, D])
        small = sb("small", [P, 3, CB])
        w_raw = sb("w_raw", [P, 2, 3 * HID])
        w_split = sb("w_split", [P, 2, 2, 3 * HID], F32R)
        bn = sb("bn", [P, 2, NB, 6])
        moments = sb("moments", [P, TB, 2])
        coef = sb("coef", [P, 7, TB])
        xnT = sb("xnT", [P, 2, T])
        wide_tiles = [sb(f"wide{n}", [P, TB, E]) for n in range(16)]
        token_tiles = [sb(f"token{n}", [P, TB]) for n in range(9)]
        expert_tiles = [sb(f"per_expert{n}", [P, E]) for n in range(5)]
        more_than = sb("more_than", [P, E, B])
        past = sb("past", [P, TILES, E])
        expert_no = sb("expert_no", [P, TILES])

        ps_turn = ctx.enter_context(nc.psum_tensor("ps_turn", [P, 2, T], F32))
        ps_logits = ctx.enter_context(nc.psum_tensor("ps_logits", [P, TB, E], F32))
        ps_within = ctx.enter_context(nc.psum_tensor("ps_within", [P, TB, E], F32))
        ps_counts = ctx.enter_context(nc.psum_tensor("ps_counts", [P, TB, E], F32))

        params = sem("r_params")
        x_loaded = [sem(f"r_x_loaded{n}") for n in range(B)]
        consts = sem("r_consts")
        bn_done = sem("bn_done")
        moments_ready = sem("moments_ready")
        coef_step = sem("coef_step")
        normed = sem("normed")
        turned = sem("r_turned")
        xnT_ready = sem("xnT_ready")
        logits_done = sem("logits_done")
        w_raw_loaded = [sem("w_raw_loaded0"), sem("w_raw_loaded1")]
        w_hi_ready = sem("w_hi_ready")
        w_lo_ready = sem("w_lo_ready")
        w_stored = [sem("w_stored0"), sem("w_stored1")]
        zeroed = sem("zeroed")
        step = sem("r_step")
        exp_ready = sem("r_exp_ready")
        counted = sem("counted")
        block = ctx.enter_context(nc.Block())
        PARAMS = 6
        STEP_DIFF = 12
        STEP_PICKED = 14

        @block.sync
        def _(sp):
            for n in range(B):
                sp.dma_start(xn[:, n * NB:(n + 1) * NB, :],
                             x[n].rearrange("(n p) d -> p n d", p=P)).then_inc(x_loaded[n], 16)
                if n == 1:
                    sp.dma_start(ident[:, :], ident_in).then_inc(params, 16)
                    sp.dma_start(w_router[:, :], router).then_inc(params, 16)
                    sp.dma_start(bias8[:, :], router_bias.partition_broadcast(P)).then_inc(params, 16)
                    sp.dma_start(rank8[:, :], rank.partition_broadcast(P)).then_inc(params, 16)
                    sp.dma_start(numbers[:, :], tile_no[0:TILES].partition_broadcast(P)).then_inc(params, 16)
                    sp.dma_start(before[:, :], tri).then_inc(params, 16)
            for e in range(2):
                sp.dma_start(w_raw[:, e, :], experts[:, e, :]).then_inc(w_raw_loaded[e], 16)
            sp.wait_ge(consts, 2)
            for i in range(TILES):
                sp.dma_start(slots_dram[i * T:(i + 1) * T].rearrange("(p n) d -> p n d", p=P),
                             zeros[:, :, :]).then_inc(zeroed, 16)
            for e in range(NE):
                sp.wait_ge(w_lo_ready, e + 1)
                sp.dma_start(weights_dram[e], w_split[:, e % 2].bitcast(F32)).then_inc(w_stored[e % 2], 16)
                if e + 2 < NE:
                    sp.dma_start(w_raw[:, e % 2, :], experts[:, e + 2, :]).then_inc(w_raw_loaded[e % 2], 16)
            sp.wait_ge(zeroed, 16 * TILES)
            for stored in w_stored:
                sp.wait_ge(stored, 8 * NE)

        @block.gpsimd
        def _(pool):
            for k, value in enumerate((-0.5, EPS, -1.0)):
                pool.memset(small[:, k, :], value)
            pool.memset(ones[:, :], 1.0).then_inc(consts, 1)
            pool.memset(zeros[:, :, :], 0.0).then_inc(consts, 1)
            pool.wait_ge(consts, 2)

            def coefficients(c):
                t = slice(c * CB, (c + 1) * CB)
                mean, var = moments[:, t, 0], moments[:, t, 1]
                ve, r, mr, bias, vr, vrr, ve2 = (coef[:, k, t] for k in range(7))
                half_, eps, minus = (small[:, k, :] for k in range(3))
                pool.wait_ge(moments_ready, (c + 1) * CB)
                for n, (dst, a, b, op) in enumerate((
                        (ve, var, eps, ALU.add), (r, ve, half_, ALU.pow), (mr, mean, r, ALU.mult),
                        (bias, mr, minus, ALU.mult), (vr, var, r, ALU.mult), (vrr, vr, r, ALU.mult),
                        (ve2, vrr, eps, ALU.add), (r2[:, t], ve2, half_, ALU.pow))):
                    pool.tensor_tensor(dst, a, b, op).then_inc(coef_step, 1)
                    pool.wait_ge(coef_step, c * 8 + n + 1)

            def split_weights(e):
                pool.wait_ge(w_hi_ready, e + 1)
                pool.tensor_tensor(w_split[:, e % 2, 1, :], w_raw[:, e % 2, :], w_split[:, e % 2, 0, :].bitcast(F32),
                                   ALU.subtract).then_inc(w_lo_ready, 1)

            for c in range(CHUNKS):
                coefficients(c)
            for e in range(NE):
                split_weights(e)

        @block.tensor
        def _(pe):
            def logits(n):
                pe.wait_ge(xnT_ready, n + 1)
                for t in range(NB):
                    mm = pe.matmul(ps_logits[:, n * NB + t, :], xnT[:, n % 2, t * P:(t + 1) * P],
                                   w_router[:, :], start=True, stop=True)
                mm.then_inc(logits_done, 1)

            pe.wait_ge(params, 16 * PARAMS)
            for n in range(B):
                pe.wait_ge(normed, (n + 1) * NB)
                if n >= 2:
                    pe.wait_ge(xnT_ready, n - 1)
                for t in range(NB):
                    mm = pe.transpose(ps_turn[:, n % 2, t * P:(t + 1) * P], xn[:, n * NB + t, :], ident[:, :])
                mm.then_inc(turned, 1)
                if n:
                    logits(n - 1)
            logits(B - 1)
            pe.wait_ge(step, STEP_PICKED)
            flat = wide_tiles[10][:, :, :].rearrange("p t e -> p (t e)")
            pe.matmul(ps_within[:, :, :].rearrange("p t e -> p (t e)"), before[:, :], flat, start=True, stop=True)
            pe.matmul(ps_counts[:, :, :].rearrange("p t e -> p (t e)"), ones[:, :], flat,
                      start=True, stop=True).then_inc(counted, 1)

        @block.scalar
        def _(act):
            def round_weights(e):
                act.wait_ge(w_raw_loaded[e % 2], 16 * (e // 2 + 1))
                if e >= 2:
                    act.wait_ge(w_stored[e % 2], 16 * (e // 2))
                act.activation(w_split[:, e % 2, 0, :], w_raw[:, e % 2, :], ACT.Copy).then_inc(w_hi_ready, 1)

            for n in range(B):
                act.wait_ge(turned, n + 1)
                if n >= 2:
                    act.wait_ge(logits_done, n - 1)
                act.activation(xnT[:, n % 2, :], ps_turn[:, n % 2, :], ACT.Copy).then_inc(xnT_ready, 1)
            for e in range(2):
                round_weights(e)
            act.wait_ge(step, STEP_DIFF)
            act.activation(token_tiles[5][:, :], token_tiles[4][:, :], ACT.Exp).then_inc(exp_ready, 1)
            for e in range(2, NE):
                round_weights(e)

        @block.vector
        def _(dve):
            def statistics(n):
                dve.wait_ge(x_loaded[n], 16)
                if n >= 2:
                    dve.wait_ge(moments_ready, (n - 1) * NB)
                for t in range(NB):
                    dve.bn_stats(bn[:, n % 2, t, :], xn[:, n * NB + t, :]).then_inc(bn_done, 1)

            def aggregate(n):
                for t in range(NB):
                    dve.wait_ge(bn_done, n * NB + t + 1)
                    dve.bn_aggr(moments[:, n * NB + t, :], bn[:, n % 2, t, :]).then_inc(moments_ready, 1)

            def normalise(n):
                dve.wait_ge(coef_step, n // CHUNK * 8 + 4)
                for t in range(n * NB, (n + 1) * NB):
                    dve.tensor_scalar(xn[:, t, :], xn[:, t, :], coef[:, 1, t:t + 1], coef[:, 3, t:t + 1],
                                      ALU.mult, ALU.add).then_inc(normed, 1)

            for c in range(CHUNKS + 1):
                for n in range(c * CHUNK, (c + 1) * CHUNK):
                    if c < CHUNKS:
                        statistics(n)
                    if c:
                        normalise(n - CHUNK)
                    if c < CHUNKS:
                        aggregate(n)

            def by_token(v):
                return v.rearrange("p (t o) -> p t o", o=1).broadcast_to([P, v.shape[1], E])

            def by_expert(v, n=TB):
                return v.rearrange("p (o e) -> p o e", o=1).broadcast_to([P, n, E])

            (logits, eq1, key1, sel1, rest, eq2, key2, sel2, slot1, slot2, both, upto, earlier, place,
             place_all, _) = (v[:, :, :] for v in wide_tiles)
            m1, k1, m2, k2, diff, e, total, s1, s2 = (v[:, :] for v in token_tiles)
            count, tiles, tiles_upto, tiles_before, first = (v[:, :] for v in expert_tiles)
            w1, w2 = (v[:, :] for v in picks)
            dve.wait_ge(params, 16 * PARAMS)
            dve.wait_ge(logits_done, B)
            scan = dve.tensor_tensor_scan
            one = ones[:, 0:TB]
            steps = [
                lambda: dve.tensor_tensor(logits, ps_logits[:, :, :], by_expert(bias8[:, :]), ALU.add),
                lambda: dve.tensor_reduce(m1, logits, AX_X, ALU.max),
                lambda: dve.tensor_tensor(eq1, logits, by_token(m1), ALU.is_equal),
                lambda: dve.tensor_tensor(key1, eq1, by_expert(rank8[:, :]), ALU.mult),
                lambda: dve.tensor_reduce(k1, key1, AX_X, ALU.max),
                lambda: dve.tensor_tensor(sel1, key1, by_token(k1), ALU.is_equal),
                lambda: dve.scalar_tensor_tensor(out=rest, in0=sel1, scalar=FAR_BELOW, in1=logits,
                                                 op0=ALU.mult, op1=ALU.add),
                lambda: dve.tensor_reduce(m2, rest, AX_X, ALU.max),
                lambda: dve.tensor_tensor(eq2, rest, by_token(m2), ALU.is_equal),
                lambda: dve.tensor_tensor(key2, eq2, by_expert(rank8[:, :]), ALU.mult),
                lambda: dve.tensor_reduce(k2, key2, AX_X, ALU.max),
                lambda: dve.tensor_tensor(diff, m2, m1, ALU.subtract),
                lambda: dve.tensor_tensor(sel2, key2, by_token(k2), ALU.is_equal),
                lambda: dve.tensor_tensor(both, sel1, sel2, ALU.add),
                lambda: dve.tensor_scalar(total, e, 1.0, None, ALU.add),
                lambda: dve.reciprocal(w1, total),
                lambda: dve.tensor_tensor(w2, e, w1, ALU.mult),
            ]
            steps += [lambda e_=e_: scan(upto[:, :, e_], one, ps_counts[:, :, e_], 0.0, ALU.mult, ALU.add)
                      for e_ in range(E)]
            steps += [
                lambda: dve.tensor_scalar(count, upto[:, TB - 1, :], 1.0 / T, None, ALU.mult),
                lambda: dve.tensor_tensor(more_than[:, :, :],
                                          count.rearrange("p (e o) -> p e o", o=1).broadcast_to([P, E, B]),
                                          numbers[:, 0:B].rearrange("p (o n) -> p o n", o=1).broadcast_to([P, E, B]),
                                          ALU.is_gt),
                lambda: dve.tensor_reduce(tiles, more_than[:, :, :], AX_X, ALU.add),
                lambda: scan(tiles_upto, ones[:, 0:E], tiles, 0.0, ALU.mult, ALU.add),
                lambda: dve.tensor_tensor(tiles_before, tiles_upto, tiles, ALU.subtract),
                lambda: dve.tensor_scalar(first, tiles_before, float(T), None, ALU.mult),
                lambda: dve.tensor_tensor(earlier, upto, ps_counts[:, :, :], ALU.subtract),
                lambda: dve.tensor_tensor(place, earlier, ps_within[:, :, :], ALU.add),
                lambda: dve.tensor_tensor(place_all, place, by_expert(first), ALU.add),
                lambda: dve.tensor_tensor(slot1, place_all, sel1, ALU.mult),
                lambda: dve.tensor_tensor(slot2, place_all, sel2, ALU.mult),
                lambda: dve.tensor_reduce(s1, slot1, AX_X, ALU.add),
                lambda: dve.tensor_reduce(s2, slot2, AX_X, ALU.add),
                lambda: dve.tensor_copy(slots[0][:, :], s1),
                lambda: dve.tensor_copy(slots[1][:, :], s2),
                lambda: dve.tensor_tensor(past[:, :, :], by_expert(tiles_upto, TILES),
                                          by_token(numbers[:, :]), ALU.is_le),
                lambda: dve.tensor_reduce(expert_no[:, :], past[:, :, :], AX_X, ALU.add),
                lambda: dve.tensor_scalar(tile_expert[:, :], expert_no[:, :], float(E - 1), None, ALU.min),
            ]
            for n, do in enumerate(steps):
                if n == STEP_PICKED:
                    dve.wait_ge(exp_ready, 1)
                if n == STEP_PICKED + 3:
                    dve.wait_ge(counted, 1)
                do().then_inc(step, 1)
                dve.wait_ge(step, n + 1)


def shared_block(nc, env):
    B, E = env["B"], env["E"]
    x, xn, base_dram, slots_dram, slots, TB = (env[k] for k in ("x", "xn", "base_dram", "slots_dram", "slots", "TB"))

    def scatter(pool, scattered):
        for t in range(TB):
            for k in range(TOP_K):
                pool.indirect_dma_start(slots_dram, bass.IndirectOffsetOnAxis(ap=slots[k][:, t:t + 1], axis=0),
                                        xn[:, t, :], None).then_inc(scattered, 16)
        pool.wait_ge(scattered, 16 * TOP_K * TB)

    NB = env["NB"]

    def tokens(n):
        return xn[:, bass.ds(n * NB, NB), :]

    def residual(n):
        src = x[n] if isinstance(n, int) else x[bass.ds(n, 1)].rearrange("o t d -> (o t) d")
        return src.rearrange("(n p) d -> p n d", p=P)

    def result(n):
        return base_dram[n] if isinstance(n, int) else base_dram[bass.ds(n, 1)].rearrange("o p n d -> (o p) n d")

    feed_forward(nc, env, "s", B, 2, tokens, result, residual=residual, meanwhile=scatter)


def routed_block(nc, env):
    slots_dram, routed_dram, T = (env[k] for k in ("slots_dram", "routed_dram", "T"))

    def rows(dram):
        return lambda n: dram[bass.ds(n * T, T)].rearrange("(n p) d -> p n d", p=P)

    feed_forward(nc, env, "t", env["TILES"], 1, rows(slots_dram), rows(routed_dram), by_tile=True)


def feed_forward(nc, env, name, rounds, per_round, tokens, result, residual=None, meanwhile=None, by_tile=False):
    T, D, NB, E, NE, HID, HC, TILES = (env[k] for k in ("T", "D", "NB", "E", "NE", "HID", "HC", "TILES"))
    weights_dram, ident, tile_expert = (env[k] for k in ("weights_dram", "ident", "tile_expert"))
    RING = 8
    U = per_round * HC
    R = RING // U
    LAG = 4
    SPLIT = 2
    D_LAG = LAG // U
    W_RING = 4 if by_tile else 1
    assert LAG % U == 0 and RING % U == 0 and SPLIT <= U and (not by_tile or R == W_RING)

    with ExitStack() as ctx:
        def sb(label, shape, dt):
            return ctx.enter_context(nc.sbuf_tensor(f"{name}_{label}", shape, dt))

        def sem(label):
            return ctx.enter_context(nc.semaphore(f"{name}_{label}"))

        def ps(label, shape):
            return ctx.enter_context(nc.psum_tensor(f"{name}_{label}", shape, F32))

        w = sb("w", [P, W_RING, per_round, 2, 3 * HID], F32R)
        xt = sb("xt", [P, 2, NB, D], F32)
        x_hi = sb("x_hi", [P, 2, T], F32R)
        x_lo = sb("x_lo", [P, 2, T], F32R)
        gate = sb("gate", [P, RING, T], F32)
        prod = sb("prod", [P, RING, T], F32)
        p_hi = sb("p_hi", [P, RING, T], F32R)
        p_lo = sb("p_lo", [P, RING, T], F32R)
        res = sb("res", [P, 2, NB, D], F32)
        yT = sb("yT", [P, T], F32)
        y_out = sb("y_out", [P, 2, NB, D], F32)
        ps_h1 = ps("ps_h1", [P, 2, T])
        ps_h3 = ps("ps_h3", [P, 2, T])
        ps_y = ps("ps_y", [P, 2, T])
        ps_in = ps("ps_in", [P, T])
        ps_out = ps("ps_out", [P, T])

        w_loaded = [sem(f"w_loaded{n}") for n in range(W_RING)]
        xt_loaded = [sem("xt_loaded0"), sem("xt_loaded1")]
        res_loaded = [sem("res_loaded0"), sem("res_loaded1")]
        x_turned = sem("x_turned")
        x_hi_ready = sem("x_hi_ready")
        x_lo_ready = sem("x_lo_ready")
        h1_ready = sem("h1_ready")
        h3_ready = sem("h3_ready")
        gate_ready = sem("gate_ready")
        prod_ready = sem("prod_ready")
        p_hi_ready = sem("p_hi_ready")
        p_lo_ready = sem("p_lo_ready")
        down_done = sem("down_done")
        yT_ready = sem("yT_ready")
        y_turned = sem("y_turned")
        y_ready = sem("y_ready")
        y_stored = [sem("y_stored0"), sem("y_stored1")]
        scattered = sem("scattered")
        block = ctx.enter_context(nc.Block())

        def each_round(eng, body, first=-1):
            last = rounds - R - rounds % R
            for n in range(first, 2 * R):
                body(n, n % R)
            with eng.Fori(2, last // R) as turn:
                for q in range(R):
                    body(turn * R + q, q)
            for n in range(last, rounds + D_LAG + 1):
                body(n, n % R)

        def exists(n):
            return not isinstance(n, int) or 0 <= n < rounds

        def later(n, k):
            return not isinstance(n, int) or n >= k

        def times(n, q, ring):
            return n // ring + 1 if isinstance(n, int) else (n - q % ring) // ring + 1

        @block.sync
        def _(sp):
            def load_tokens(n, q):
                if later(n, 2):
                    sp.wait_ge(x_turned, n - 1)
                sp.dma_start(xt[:, q % 2], tokens(n)).then_inc(xt_loaded[q % 2], 16)

            def load_residual(n, q):
                if later(n, 2):
                    sp.wait_ge(y_ready, n - 1)
                sp.dma_start(res[:, q % 2], residual(n)).then_inc(res_loaded[q % 2], 16)

            def load_weights(n, q):
                if later(n, W_RING):
                    sp.wait_ge(down_done, (n - (W_RING - 1)) * U)
                e = sp.value_load(tile_expert[0:1, bass.ds(n, 1)], min_val=0, max_val=E - 1)
                sp.dma_start(w[:, q, 0].bitcast(F32),
                             weights_dram[bass.ds(e, 1)].rearrange("o p k c -> (o p) k c")).then_inc(w_loaded[q], 16)

            if not by_tile:
                for e in range(E, NE):
                    sp.dma_start(w[:, 0, e - E].bitcast(F32), weights_dram[e]).then_inc(w_loaded[0], 16)

            def body(n, q):
                if exists(n + 2):
                    load_tokens(n + 2, (q + 2) % R)
                if by_tile and exists(n + 2):
                    load_weights(n + 2, (q + 2) % R)
                if residual and exists(n - D_LAG):
                    load_residual(n - D_LAG, (q - D_LAG) % R)
                done = n - 1 - D_LAG
                if exists(done):
                    sp.wait_ge(y_ready, done + 1)
                    sp.dma_start(result(done), y_out[:, (q - 1 - D_LAG) % 2]).then_inc(y_stored[(q - 1 - D_LAG) % 2], 16)

            each_round(sp, body, -2)
            for k, stored in enumerate(y_stored):
                sp.wait_ge(stored, 16 * ((rounds + 1 - k) // 2))

        if meanwhile:
            @block.gpsimd
            def _(pool):
                meanwhile(pool, scattered)

        @block.tensor
        def _(pe):
            def turn_in(n, q):
                pe.wait_ge(xt_loaded[q % 2], times(n, q, 2) * 16)
                if later(n, 1):
                    pe.wait_ge(x_lo_ready, n)
                for t in range(NB):
                    mm = pe.transpose(ps_in[:, t * P:(t + 1) * P], xt[:, q % 2, t, :], ident[:, :])
                mm.then_inc(x_turned, 1)

            def turn_out(n):
                pe.wait_ge(yT_ready, n + 1)
                if later(n, 1):
                    pe.wait_ge(y_ready, n)
                for t in range(NB):
                    mm = pe.transpose(ps_out[:, t * P:(t + 1) * P], yT[:, t * P:(t + 1) * P], ident[:, :])
                mm.then_inc(y_turned, 1)

            def up(n, q, u):
                e, hc = u // HC, u % HC
                N = n * U + u
                if u == 0:
                    pe.wait_ge(x_lo_ready, n + 1)
                    if by_tile:
                        pe.wait_ge(w_loaded[q], times(n, q, W_RING) * 16)
                for third, bank, ready in ((0, ps_h1[:, u % 2, :], h1_ready), (1, ps_h3[:, u % 2, :], h3_ready)):
                    if not (isinstance(N, int) and N < 2):
                        pe.wait_ge(prod_ready if third else gate_ready, N - 1)
                    cols = slice(third * HID + hc * P, third * HID + (hc + 1) * P)
                    w_hi, w_lo = (w[:, q % W_RING, e, k, cols] for k in range(2))
                    pe.matmul(bank, w_hi, x_hi[:, q % 2, :], start=True, stop=False)
                    pe.matmul(bank, w_hi, x_lo[:, q % 2, :], start=False, stop=False)
                    pe.matmul(bank, w_lo, x_hi[:, q % 2, :], start=False, stop=True).then_inc(ready, 1)

            def down(n, q, u):
                e, hc = u // HC, u % HC
                pe.wait_ge(p_lo_ready, n * U + (u + 1))
                if u == 0 and later(n, 2):
                    pe.wait_ge(yT_ready, n - 1)
                cols = slice(2 * HID + hc * P, 2 * HID + (hc + 1) * P)
                w_hi, w_lo = (w[:, q % W_RING, e, k, cols] for k in range(2))
                bank, r = ps_y[:, q % 2, :], (q * U + u) % RING
                pe.matmul(bank, w_hi, p_hi[:, r, :], start=(u == 0), stop=False)
                pe.matmul(bank, w_hi, p_lo[:, r, :], start=False, stop=False)
                pe.matmul(bank, w_lo, p_hi[:, r, :], start=False, stop=(u == U - 1)).then_inc(down_done, 1)

            def body(n, q):
                if exists(n + 1):
                    turn_in(n + 1, (q + 1) % R)
                for u in range(U):
                    if exists(n):
                        up(n, q, u)
                    if u == U - 1 and exists(n - 1 - D_LAG):
                        turn_out(n - 1 - D_LAG)
                    if exists(n - D_LAG):
                        down(n - D_LAG, (q - D_LAG) % R, u)

            if not by_tile:
                pe.wait_ge(w_loaded[0], 16 * (NE - E))
            each_round(pe, body)

        @block.scalar
        def _(act):
            def round_x(n, q):
                act.wait_ge(x_turned, n + 1)
                if later(n, 2):
                    act.wait_ge(h3_ready, (n - 1) * U)
                act.activation(x_hi[:, q % 2, :], ps_in[:, :], ACT.Copy).then_inc(x_hi_ready, 1)

            def silu(n, q, u):
                N = n * U + u
                act.wait_ge(h1_ready, N + 1)
                if not (isinstance(N, int) and N < RING):
                    act.wait_ge(prod_ready, N - (RING - 1))
                act.activation(gate[:, (q * U + u) % RING, :], ps_h1[:, u % 2, :], ACT.Silu).then_inc(gate_ready, 1)

            def round_product(N, r):
                act.wait_ge(prod_ready, N + 1)
                if not (isinstance(N, int) and N < RING):
                    act.wait_ge(down_done, N - (RING - 1))
                act.activation(p_hi[:, r, :], prod[:, r, :], ACT.Copy).then_inc(p_hi_ready, 1)

            def read_y(n, q):
                act.wait_ge(down_done, n * U + U)
                if later(n, 1):
                    act.wait_ge(y_turned, n)
                act.activation(yT[:, :], ps_y[:, q % 2, :], ACT.Copy).then_inc(yT_ready, 1)

            def body(n, q):
                for u in range(U):
                    if exists(n):
                        silu(n, q, u)
                    if u == 0 and exists(n + 1):
                        round_x(n + 1, (q + 1) % R)
                    if u == 0 and exists(n - 1 - D_LAG):
                        read_y(n - 1 - D_LAG, (q - 1 - D_LAG) % R)
                    N = n * U + (u - SPLIT)
                    if not isinstance(n, int) or 0 <= N < rounds * U:
                        round_product(N, (q * U + u - SPLIT) % RING)

            each_round(act, body)

        @block.vector
        def _(dve):
            def split_x(n, q):
                dve.wait_ge(x_hi_ready, n + 1)
                dve.tensor_tensor(x_lo[:, q % 2, :], ps_in[:, :], x_hi[:, q % 2, :].bitcast(F32),
                                  ALU.subtract).then_inc(x_lo_ready, 1)

            def multiply(n, q, u):
                N = n * U + u
                r = (q * U + u) % RING
                dve.wait_ge(gate_ready, N + 1)
                dve.wait_ge(h3_ready, N + 1)
                if not (isinstance(N, int) and N < RING):
                    dve.wait_ge(p_lo_ready, N - (RING - 1))
                dve.tensor_tensor(prod[:, r, :], ps_h3[:, u % 2, :], gate[:, r, :], ALU.mult).then_inc(prod_ready, 1)

            def split_product(N, r):
                dve.wait_ge(p_hi_ready, N + 1)
                if not (isinstance(N, int) and N < RING):
                    dve.wait_ge(down_done, N - (RING - 1))
                dve.tensor_tensor(p_lo[:, r, :], prod[:, r, :], p_hi[:, r, :].bitcast(F32),
                                  ALU.subtract).then_inc(p_lo_ready, 1)

            def finish(n, q):
                dve.wait_ge(y_turned, n + 1)
                if later(n, 2):
                    dve.wait_ge(y_stored[q % 2], (times(n, q, 2) - 1) * 16)
                src = ps_out[:, :].rearrange("p (n d) -> p n d", d=D)
                if residual:
                    dve.wait_ge(res_loaded[q % 2], times(n, q, 2) * 16)
                    dve.tensor_tensor(y_out[:, q % 2], src, res[:, q % 2], ALU.add).then_inc(y_ready, 1)
                else:
                    dve.tensor_copy(y_out[:, q % 2], src).then_inc(y_ready, 1)

            def body(n, q):
                for u in range(U):
                    if exists(n):
                        multiply(n, q, u)
                    if u == 0 and exists(n + 1):
                        split_x(n + 1, (q + 1) % R)
                    N = n * U + (u - SPLIT)
                    if not isinstance(n, int) or 0 <= N < rounds * U:
                        split_product(N, (q * U + u - SPLIT) % RING)
                    if u == U - 1 and exists(n - 1 - D_LAG):
                        finish(n - 1 - D_LAG, (q - 1 - D_LAG) % R)

            each_round(dve, body)

def kernel(**inputs):
    import numpy as np
    import concourse.bacc as bacc
    from concourse.bass_utils import run_bass_kernel_spmd as run

    a = {k.replace("L0_attn_", "a_").replace("L0_ffn_", "f_"): np.asarray(v) for k, v in inputs.items()}
    x = np.ascontiguousarray(a["a_x"])
    D = x.shape[2]

    def first_layer(w):
        return w.transpose(2, 0, 1)

    def second_layer(w):
        n, d, h = w.shape
        return w.reshape(n, d, h // 128, 128).transpose(3, 0, 2, 1).reshape(128, n, h)

    every = {k: np.concatenate([a["f_" + k], a["f_s" + k]]) for k in ("w1", "w3", "w2")}
    laid = {
        "x": x,
        "vecs": np.stack([a[k] for k in ("a_ln_g", "a_ln_b", "a_bq", "a_bk", "a_bv")], 1),
        "wqkv": np.stack([a["a_Wq"], a["a_Wk"], a["a_Wv"]], 1),
        "experts": np.concatenate(
            [first_layer(every["w1"]), first_layer(every["w3"]), second_layer(every["w2"])], 2),
        "router": a["f_router_w"].T,
        "router_bias": a["f_expert_bias"],
        "rank": np.arange(a["f_router_w"].shape[0], 0, -1).astype(np.float32),
        "tile_no": np.arange(2 * x.shape[0] + 8, dtype=np.float32),
        "tri": np.triu(np.ones((D, D), np.float32), 1),
        "ident_in": np.eye(D, dtype=np.float32),
    }
    nc = bacc.Bacc("TRN2", target_bir_lowering=False, num_devices=1)
    arrays, args = {}, []
    for name, v in laid.items():
        v = np.ascontiguousarray(v)
        arrays[f"{name}_dram"] = v
        args.append(nc.dram_tensor(f"{name}_dram", v.shape, mybir.dt.from_np(v.dtype), kind="ExternalInput").ap())
    args.append(nc.dram_tensor("out_dram", x.shape, F32, kind="ExternalOutput").ap())
    prenorm_attention_moe(nc, *args)
    r = run(nc, [arrays], core_ids=[0])
    return r.results[0]["out_dram"]
```

```python
from contextlib import ExitStack

import concourse.bass as bass
from concourse import mybir

F32 = mybir.dt.float32
F32R = mybir.dt.float32r
U32 = mybir.dt.uint32
ALU = mybir.AluOpType
ACT = mybir.ActivationFunctionType
AX_X = mybir.AxisListType.X

P = 128
EPS = 1e-5
TERMS = 4
GROUP = 4
HI_SLOTS_Q = (0, 1)
LO_SLOT_Q = 2
HI_SLOTS_K = (0, 2)
LO_SLOT_K = 1
SHIFT_SLOT = 3
PROBS_RING = 4
TOP_K = 2
BANKS = 3
FAR_BELOW = -3.0e38


def prenorm_attention_moe(nc, x, vecs, wqkv, experts, router, router_bias, rank, tile_no, tri, ident_in, out):
    B, T, D = x.shape
    E = router.shape[1]
    NE = experts.shape[1]
    HID = experts.shape[2] // 3
    NB = T // P
    TB = B * NB
    HC = HID // P
    HEADS = 16
    DH = D // HEADS
    GROUPS = HEADS // GROUP
    SCALE = float(DH) ** -0.5
    ROWS = DH * TERMS
    G_ALL = B * GROUPS
    TILES = (TOP_K * B * T + E * (T - 1)) // T
    SPARE = TILES - TOP_K * B
    REGION = B * T + T
    SLOTS = E * REGION + SPARE * T
    assert D == P and ROWS * GROUP == P and T == 512 and B % 2 == 0 and GROUPS == 4 and NB == 4
    assert tile_no.shape[0] >= TILES >= B

    def scratch(name, shape):
        return nc.dram_tensor(name, shape, F32, kind="Internal").ap()

    slots_dram = scratch("slots_dram", [SLOTS, D])
    routed_dram = scratch("routed_dram", [TILES * T, D])
    base_dram = scratch("base_dram", [B, P, NB, D])

    with ExitStack() as outer:
        def keep(name, shape, dt):
            return outer.enter_context(nc.sbuf_tensor(name, shape, dt))

        ident = keep("ident", [P, P], F32)
        xn = keep("xn", [P, TB, D], F32)
        r2 = keep("r2", [P, TB], F32)
        picks = [keep(f"pick{k}", [P, TB], F32) for k in range(TOP_K)]
        slots = [keep(f"slot{k}", [P, TB], U32) for k in range(TOP_K)]
        tile_expert = keep("tile_expert", [P, TILES], U32)
        tile_slot = keep("tile_slot", [P, TILES], U32)
        logits = keep("logits", [P, TB, E], F32)
        rank8 = keep("rank8", [P, E], F32)
        numbers = keep("numbers", [P, TILES], F32)
        before = keep("before", [P, P], F32)
        ones = keep("ones", [P, P], F32)
        zeros = keep("zeros", [P, NB, D], F32)
        shared_w = keep("shared_w", [P, 1, 2, NE - E, 3 * HID], F32R)
        env = locals()
        with nc.sbuf_tensor("xnT", [P, B, T], F32) as xnT:
            route_block(nc, {**env, "xnT": xnT})
            shared_block(nc, {**env, "xnT": xnT})
        routed_block(nc, env)
        attention_block(nc, env)


def attention_block(nc, env):
    vecs, wqkv, out = (env[k] for k in ("vecs", "wqkv", "out"))
    B, T, D, NB, NE, HID, DH, HEADS, GROUPS, ROWS, G_ALL, SCALE = (
        env[k] for k in ("B", "T", "D", "NB", "NE", "HID", "DH", "HEADS", "GROUPS", "ROWS", "G_ALL", "SCALE"))
    routed_dram, base_dram, ident, xn_all, r2_all, picks, slots = (
        env[k] for k in ("routed_dram", "base_dram", "ident", "xn", "r2", "picks", "slots"))
    LAST_PREP = B - 2

    with ExitStack() as ctx:
        def sb(name, shape, dt):
            return ctx.enter_context(nc.sbuf_tensor(name, shape, dt))

        def sem(name):
            return ctx.enter_context(nc.semaphore(name))

        vec = sb("vec", [P, 5], F32)
        bq_scaled = sb("bq_scaled", [P, 1], F32)
        wp_raw = sb("wp_raw", [P, 3, D], F32)
        wp_hi = sb("wp_hi", [P, 3, D], F32R)
        wp_lo = sb("wp_lo", [P, 3, D], F32R)
        xn = sb("xn_tile", [P, 2, NB, D], F32)
        xa = sb("xa", [P, NB, D], F32)
        r2 = sb("r2_tile", [P, NB], F32)
        slot = sb("slot_tile", [P, TOP_K, NB], U32)
        pick = sb("pick_tile", [P, TOP_K, NB], F32)
        routed = sb("routed", [P, TOP_K, NB, D], F32)
        base = sb("base", [P, 2, NB, D], F32)
        total = sb("total", [P, 2, NB, D], F32)
        xaT = sb("xaT", [P, T], F32)
        xaT_hi = sb("xaT_hi", [P, T], F32R)
        xaT_lo = sb("xaT_lo", [P, T], F32R)
        qT = sb("qT", [P, T], F32)
        kT = sb("kT", [P, T], F32)
        vT = sb("vT", [P, T], F32)
        q_terms = sb("q_terms", [P, 2, TERMS, T], F32R)
        k_terms = sb("k_terms", [P, 2, TERMS, T], F32R)
        q_stack = sb("q_stack", [P, GROUPS, GROUP, T], F32R)
        k_stack = sb("k_stack", [P, GROUPS, T], F32R)
        v_one = sb("v_one", [P, 2, NB, HEADS, DH + 1], F32)
        maxima = sb("maxima", [P, 2, GROUP * NB], F32)
        shift = sb("shift", [GROUP * NB, 2, P], F32R)
        probs = sb("probs", [P, PROBS_RING, GROUP, T], F32)
        oT = sb("oT", [P, T], F32)
        recip = sb("recip", [P, NB, GROUP], F32)
        fence = sb("fence", [P, 1], F32)
        attn = sb("attn", [P, 2, NB, D], F32)

        ps_scores = ctx.enter_context(nc.psum_tensor("ps_scores", [P, BANKS, T], F32))
        ps_scoresT = ctx.enter_context(nc.psum_tensor("ps_scoresT", [P, BANKS, T], F32))
        ps_out = ctx.enter_context(nc.psum_tensor("ps_out", [P, T], F32))
        ps_misc = ctx.enter_context(nc.psum_tensor("ps_misc", [P, T], F32))

        params_loaded = sem("params_loaded")
        consts_ready = sem("consts_ready")
        pool_consts = sem("pool_consts")
        dve_cleared = sem("dve_cleared")
        xn_loaded = [sem("xn_loaded0"), sem("xn_loaded1")]
        r2_taken = sem("r2_taken")
        xa_ready = sem("xa_ready")
        picked = sem("picked")
        gathered = [sem("gathered0"), sem("gathered1")]
        base_loaded = [sem("base_loaded0"), sem("base_loaded1")]
        total_step = sem("total_step")
        total_stored = [sem("total_stored0"), sem("total_stored1")]
        misc_filled = sem("misc_filled")
        misc_emptied = sem("misc_emptied")
        xa_hi_ready = sem("xa_hi_ready")
        xa_lo_ready = sem("xa_lo_ready")
        hi_terms = sem("hi_terms")
        lo_terms = sem("lo_terms")
        stacks_loaded = [sem(f"stacks_loaded{g}") for g in range(GROUPS)]
        scores_ready = sem("scores_ready")
        maxima_ready = sem("maxima_ready")
        shift_loaded = sem("shift_loaded")
        scoresT_ready = sem("scoresT_ready")
        probs_ready = sem("probs_ready")
        pv_done = sem("pv_done")
        oT_ready = sem("oT_ready")
        recip_ready = sem("recip_ready")

        PARAM_DMAS = 2
        TOTAL = TOP_K + 3
        USES = 2 * GROUPS + 5
        block = ctx.enter_context(nc.Block())

        LEAD_USES = 10
        LEAD_M = 5
        PREP_BEFORE = (0, 1, 2, 4)

        def misc_before(b, g):
            if not isinstance(b, int):
                return b * USES + (LEAD_USES + 2 * g - 1 + PREP_BEFORE[g])
            G = b * GROUPS + g
            prep = 5 * min(b, LAST_PREP)
            if b < LAST_PREP:
                prep += PREP_BEFORE[g]
            elif b == LAST_PREP:
                prep += 1 if g else 0
            else:
                prep += 1
            return LEAD_USES + max(G - 1, 0) + min(G, G_ALL - 1) + prep

        def use_m(b, g):
            return misc_before(b, g)

        def use_t(b, g):
            last = isinstance(b, int) and b == B - 1 and g == GROUPS - 1
            return misc_before(b, g) + (0 if last else 1)

        def use_prep(b, g, n):
            first = isinstance(b, int) and b == 0 and g == 0
            return misc_before(b, g) + (1 if first else 2) + n

        def use_of(kind, n):
            lead = {"xa": 0, "q": 1, "k": 2, "v": 3, "vt": 4}[kind]
            if isinstance(n, int) and n == 0:
                return lead
            if kind == "vt":
                return use_prep(n - 1, 0, 0)
            if isinstance(n, int) and n == 1:
                return LEAD_M + 1 + lead
            g, k = {"xa": (1, 0), "q": (2, 0), "k": (2, 1), "v": (3, 0)}[kind]
            return use_prep(n - 2, g, k)

        def bank(g, par, k):
            ring = 2 * GROUPS * GROUP * NB
            at = (par * GROUPS + g) * GROUP * NB + k
            if at >= BANKS:
                return at % BANKS, BANKS
            last = max(v for v in range(ring) if v % BANKS == at)
            return at, at + ring - last

        def batches(eng, body):
            body(0, 0)
            body(1, 1)
            with eng.Fori(1, B // 2 - 1) as pair:
                body(pair * 2, 0)
                body(pair * 2 + 1, 1)
            body(B - 2, 0)
            body(B - 1, 1)

        def at_start(b, g=0):
            return isinstance(b, int) and b == 0 and g == 0

        def at_end(b, g=3):
            return isinstance(b, int) and b == B - 1 and g == GROUPS - 1

        def prepares(b):
            return not isinstance(b, int) or b < LAST_PREP

        def has_next(b):
            return not isinstance(b, int) or b < B - 1

        def half(b, par):
            return b // 2 if isinstance(b, int) else (b - par) // 2

        @block.sync
        def _(sp):
            def load_xn(n, par):
                if not (isinstance(n, int) and n < 3):
                    sp.wait_ge(xa_ready, n - 1)
                src = xn_all[:, bass.ds(n * NB, NB), :]
                sp.dma_start(xn[:, par], src).then_inc(xn_loaded[par], 16)

            sp.dma_start(vec[:, :], vecs).then_inc(params_loaded, 16)
            sp.dma_start(wp_raw[:, :, :], wqkv).then_inc(params_loaded, 16)

            def load_base(n, par):
                if not (isinstance(n, int) and n < 2):
                    sp.wait_ge(total_step, (n - 1) * TOTAL)
                src = base_dram[n] if isinstance(n, int) else base_dram[bass.ds(n, 1)].rearrange("o p n d -> (o p) n d")
                sp.dma_start(base[:, par], src).then_inc(base_loaded[par], 16)

            def store_total(n, par):
                sp.wait_ge(total_step, n * TOTAL + TOTAL)
                dst = out[n] if isinstance(n, int) else out[bass.ds(n, 1)].rearrange("o t d -> (o t) d")
                sp.dma_start(dst.rearrange("(n p) d -> p n d", p=P), total[:, par]).then_inc(total_stored[par], 16)

            def load_stacks(n, par, g, freed):
                sp.wait_ge(lo_terms, n * 2 + 2)
                if freed is not None:
                    sp.wait_ge(scoresT_ready, freed)
                rows = GROUP * DH
                sp.dma_start(k_stack[:, g, :].bitcast(F32),
                             k_terms[g * rows:(g + 1) * rows, par].bitcast(F32)).then_inc(stacks_loaded[g], 16)
                for j in range(GROUP):
                    h = g * GROUP + j
                    sp.dma_start(q_stack[j * ROWS:(j + 1) * ROWS, g, j, :].bitcast(F32),
                                 q_terms[h * DH:(h + 1) * DH, par].bitcast(F32)).then_inc(stacks_loaded[g], 16)

            def load_shift(g, par, emptied):
                sp.wait_ge(misc_emptied, emptied)
                for j in range(GROUP):
                    row = j * ROWS + SHIFT_SLOT
                    sp.dma_start(q_stack[row:row + 1, g, j, :].bitcast(F32),
                                 shift[j * NB:(j + 1) * NB, par, :].bitcast(F32)).then_inc(shift_loaded, 16)

            load_xn(1, 1)
            load_base(0, 0)
            sp.wait_ge(pool_consts, 1)
            for g in range(GROUPS):
                if g < 2:
                    sp.wait_ge(dve_cleared, g + 1)
                else:
                    sp.wait_ge(pool_consts, g)
                load_stacks(0, 0, g, None)
            load_shift(0, 0, LEAD_M + 1)

            def body(b, par):
                for g in range(GROUPS):
                    G = b * GROUPS + g
                    if g == 0 and prepares(b):
                        load_xn(b + 2, par)
                    if not at_end(b, g):
                        load_shift((g + 1) % GROUPS, (g + 1) % 2, use_m(b, g) + 1)
                    if g == 1 and has_next(b):
                        load_base(b + 1, 1 - par)
                    if g == 2 and not (isinstance(b, int) and b == 0):
                        store_total(b - 1, 1 - par)
                    if has_next(b):
                        load_stacks(b + 1, 1 - par, g, (G + 1) * (GROUP * NB))

            batches(sp, body)
            store_total(B - 1, (B - 1) % 2)
            for stored in total_stored:
                sp.wait_ge(stored, 8 * B)

        @block.gpsimd
        def _(pool):
            def wide(v):
                return v.rearrange("p (n o) -> p n o", o=1).broadcast_to([P, NB, D])

            def take_r2(n):
                pool.tensor_copy(r2[:, :], r2_all[:, bass.ds(n * NB, NB)]).then_inc(r2_taken, 1)

            def scale_xn(n, par):
                pool.wait_ge(r2_taken, n)
                pool.wait_ge(misc_filled, use_of("xa", n - 1) + 1)
                pool.wait_ge(xn_loaded[par], (half(n, par) + par) * 16)
                pool.tensor_tensor(xa[:, :, :], xn[:, par], wide(r2[:, :]), ALU.mult).then_inc(xa_ready, 1)

            def take_picks(n):
                for k in range(TOP_K):
                    pool.tensor_copy(slot[:, k, :], slots[k][:, bass.ds(n * NB, NB)]).then_inc(picked, 1)
                    pool.tensor_copy(pick[:, k, :], picks[k][:, bass.ds(n * NB, NB)]).then_inc(picked, 1)

            def gather(n):
                pool.wait_ge(picked, n * (2 * TOP_K) + 2 * TOP_K)
                pool.tensor_tensor(fence[:, :], fence[:, :], fence[:, :], ALU.mult)
                for k in range(TOP_K):
                    for t in range(NB):
                        pool.indirect_dma_start(routed[:, k, t, :], None, routed_dram,
                                                bass.IndirectOffsetOnAxis(ap=slot[:, k, t:t + 1], axis=0)
                                                ).then_inc(gathered[k], 16)

            def add_up(n, par):
                step = n * TOTAL
                for k in range(TOP_K):
                    pool.wait_ge(gathered[k], n * (16 * NB) + 16 * NB)
                    pool.tensor_tensor(routed[:, k], routed[:, k], wide(pick[:, k, :]), ALU.mult).then_inc(total_step, 1)
                pool.wait_ge(base_loaded[par], (half(n, par) + 1) * 16)
                if not (isinstance(n, int) and n < 2):
                    pool.wait_ge(total_stored[par], half(n, par) * 16)
                pool.wait_ge(total_step, step + TOP_K)
                pool.tensor_tensor(total[:, par], routed[:, 0], routed[:, 1], ALU.add).then_inc(total_step, 1)
                pool.wait_ge(total_step, step + (TOP_K + 1))
                pool.tensor_tensor(total[:, par], total[:, par], base[:, par], ALU.add).then_inc(total_step, 1)
                last = misc_before(B - 1, GROUPS - 1) + 2 if isinstance(n, int) and n == B - 1 else use_t(n + 1, 0) + 1
                pool.wait_ge(misc_emptied, last)
                pool.wait_ge(total_step, step + (TOP_K + 2))
                pool.tensor_tensor(total[:, par], total[:, par], attn[:, par], ALU.add).then_inc(total_step, 1)

            def split_xa(n):
                pool.wait_ge(xa_hi_ready, n + 1)
                if not (isinstance(n, int) and n == 0):
                    pool.wait_ge(misc_filled, use_of("v", n - 1) + 1)
                pool.tensor_tensor(xaT_lo[:, :], xaT[:, :], xaT_hi[:, :].bitcast(F32),
                                   ALU.subtract).then_inc(xa_lo_ready, 1)

            def split_qk(n, par):
                pool.wait_ge(hi_terms, n * 2 + 1)
                pool.tensor_tensor(q_terms[:, par, LO_SLOT_Q, :], qT[:, :],
                                   q_terms[:, par, HI_SLOTS_Q[0], :].bitcast(F32), ALU.subtract).then_inc(lo_terms, 1)
                pool.wait_ge(hi_terms, n * 2 + 2)
                pool.tensor_tensor(k_terms[:, par, LO_SLOT_K, :], kT[:, :],
                                   k_terms[:, par, HI_SLOTS_K[0], :].bitcast(F32), ALU.subtract).then_inc(lo_terms, 1)

            pool.tensor_tensor(xa[:, :, :], xn_all[:, 0:NB, :], wide(r2_all[:, 0:NB]), ALU.mult).then_inc(xa_ready, 1)
            pool.memset(fence[:, :], 0.0)
            pool.memset(q_terms[:, :, SHIFT_SLOT, :].bitcast(F32), 0.0)
            pool.memset(k_terms[:, :, SHIFT_SLOT, :].bitcast(F32), 1.0).then_inc(pool_consts, 1)
            for n in range(2):
                if n:
                    take_r2(n)
                    scale_xn(n, n)
                pool.memset(q_stack[:, n + 2].bitcast(F32), 0.0).then_inc(pool_consts, 1)
                split_xa(n)
                if n == 0:
                    pool.wait_ge(pool_consts, 1)
                split_qk(n, n)

            def body(b, par):
                if not (isinstance(b, int) and b == 0):
                    take_picks(b - 1)
                if prepares(b):
                    take_r2(b + 2)
                if not (isinstance(b, int) and b == 0):
                    gather(b - 1)
                if prepares(b):
                    scale_xn(b + 2, par)
                if not (isinstance(b, int) and b == 0):
                    add_up(b - 1, 1 - par)
                if prepares(b):
                    split_xa(b + 2)
                    split_qk(b + 2, par)

            batches(pool, body)
            take_picks(B - 1)
            gather(B - 1)
            add_up(B - 1, (B - 1) % 2)

        @block.tensor
        def _(pe):
            def begin(use):
                if not (isinstance(use, int) and use == 0):
                    pe.wait_ge(misc_emptied, use)

            def turn_blocks(use, src):
                begin(use)
                for t in range(NB):
                    last = pe.transpose(ps_misc[:, t * P:(t + 1) * P], src[:, t, :], ident[:, :])
                last.then_inc(misc_filled, 1)

            def prep(kind, n):
                use = use_of(kind, n)
                if kind == "xa":
                    pe.wait_ge(xa_ready, n + 1)
                    turn_blocks(use, xa)
                elif kind == "vt":
                    pe.wait_ge(misc_emptied, use_of("v", n) + 1)
                    turn_blocks(use, vT[:, :].rearrange("p (n q) -> p n q", q=P))
                else:
                    w = "qkv".index(kind)
                    pe.wait_ge(xa_lo_ready, n + 1)
                    begin(use)
                    pe.matmul(ps_misc[:, :], wp_hi[:, w, :], xaT_hi[:, :], start=True, stop=False)
                    pe.matmul(ps_misc[:, :], wp_hi[:, w, :], xaT_lo[:, :], start=False, stop=False)
                    pe.matmul(ps_misc[:, :], wp_lo[:, w, :], xaT_hi[:, :], start=False,
                              stop=True).then_inc(misc_filled, 1)

            def scores(G, g, par, k):
                j, n = k // NB, k % NB
                at, back = bank(g, par, k)
                if not (isinstance(G, int) and G * 16 + k < BANKS):
                    pe.wait_ge(maxima_ready, G * 16 + (k + 1 - back))
                pe.matmul(ps_scores[:, at, :], q_stack[:, g, j, n * P:(n + 1) * P],
                          k_stack[:, g, :], start=True, stop=True).then_inc(scores_ready, 1)

            def scoresT(G, g, par, k):
                m, j = k // GROUP, k % GROUP
                at, back = bank(g, par, k)
                if not (isinstance(G, int) and G * 16 + k < BANKS):
                    pe.wait_ge(probs_ready, G * 16 + (k + 1 - back))
                pe.matmul(ps_scoresT[:, at, :], k_stack[:, g, m * P:(m + 1) * P],
                          q_stack[:, g, j, :], start=True, stop=True).then_inc(scoresT_ready, 1)

            def values(G, g, par, m):
                pe.wait_ge(probs_ready, G * 16 + (m + 1) * GROUP)
                if m == 0 and not (isinstance(G, int) and G == 0):
                    pe.wait_ge(oT_ready, G)
                for j in range(GROUP):
                    mm = pe.matmul(ps_out[j * ROWS:j * ROWS + DH + 1, :], v_one[:, par, m, g * GROUP + j, :],
                                   probs[:, m, j, :], start=(m == 0), stop=(m == NB - 1),
                                   tile_position=(0, j * ROWS))
                mm.then_inc(pv_done, 1)

            def turn_maxima(use, G, par):
                pe.wait_ge(maxima_ready, G * 16 + 16)
                begin(use)
                pe.transpose(ps_misc[0:GROUP * NB, 0:P], maxima[:, par, :], ident[:, :]).then_inc(misc_filled, 1)

            def turn_output(use, G):
                pe.wait_ge(oT_ready, G + 1)
                turn_blocks(use, oT[:, :].rearrange("p (n q) -> p n q", q=P))

            prep("xa", 0)
            pe.wait_ge(params_loaded, 16 * PARAM_DMAS)
            pe.wait_ge(consts_ready, 3)
            for kind in ("q", "k", "v", "vt"):
                prep(kind, 0)
            for G in range(2):
                pe.wait_ge(stacks_loaded[G], 80)
                for k in range(GROUP * NB):
                    scores(G, G, 0, k)
                    if (G, k) == (1, 2):
                        turn_maxima(LEAD_M, 0, 0)
                    kind = {(1, 4): "xa", (1, 9): "q", (1, 12): "k", (1, 15): "v"}.get((G, k))
                    if kind:
                        prep(kind, 1)

            def body(b, par):
                for g in range(GROUPS):
                    G = b * GROUPS + g
                    ahead = not isinstance(b, int) or G + 2 < G_ALL
                    pe.wait_ge(shift_loaded, G * (16 * GROUP) + 16 * GROUP)
                    if ahead:
                        g2 = (g + 2) % GROUPS
                        pe.wait_ge(stacks_loaded[g2], (b + (1 + (g + 2) // GROUPS)) * 80)
                    for m in range(NB):
                        for k in range(m * GROUP, (m + 1) * GROUP):
                            scoresT(G, g, par, k)
                            if ahead:
                                scores(G + 2, g2, par if g < 2 else 1 - par, k)
                        if m > 0:
                            values(G, g, par, m - 1)
                        elif not at_start(b, g):
                            values(G - 1, (g - 1) % GROUPS, par if g else 1 - par, NB - 1)
                        if m == 0 and not at_end(b, g):
                            turn_maxima(use_m(b, g), G + 1, (g + 1) % 2)
                        if m == 1 and not at_start(b, g):
                            turn_output(use_t(b, g), G - 1)
                        if m == 2 and g == 0 and has_next(b):
                            prep("vt", b + 1)
                        if m >= 2 and g and prepares(b):
                            kind = {(1, 3): "xa", (2, 2): "q", (2, 3): "k", (3, 2): "v"}.get((g, m))
                            if kind:
                                prep(kind, b + 2)

            batches(pe, body)
            values(G_ALL - 1, GROUPS - 1, (B - 1) % 2, NB - 1)
            turn_output(misc_before(B - 1, GROUPS - 1) + 1, G_ALL - 1)

        @block.scalar
        def _(act):
            act.wait_ge(params_loaded, 16 * PARAM_DMAS)

            def empty(kind, n):
                use = use_of(kind, n)
                act.wait_ge(misc_filled, use + 1)
                first = isinstance(n, int) and n == 0
                if kind == "xa":
                    if not first:
                        act.wait_ge(xa_lo_ready, n)
                    op = act.activation(xaT[:, :], ps_misc[:, :], ACT.Identity, bias=vec[:, 1:2], scale=vec[:, 0:1])
                elif kind == "q":
                    if not first:
                        act.wait_ge(lo_terms, n * 2 - 1)
                    op = act.activation(qT[:, :], ps_misc[:, :], ACT.Identity, bias=bq_scaled[:, :], scale=SCALE)
                elif kind == "k":
                    if not first:
                        act.wait_ge(lo_terms, n * 2)
                    op = act.activation(kT[:, :], ps_misc[:, :], ACT.Identity, bias=vec[:, 3:4])
                else:
                    op = act.activation(vT[:, :], ps_misc[:, :], ACT.Identity, bias=vec[:, 4:5])
                op.then_inc(misc_emptied, 1)

            def place_values(n, par):
                act.wait_ge(misc_filled, use_of("vt", n) + 1)
                act.activation(v_one[:, par, :, :, 0:DH], ps_misc[:, :].rearrange("p (n h d) -> p n h d", n=NB, d=DH),
                               ACT.Copy).then_inc(misc_emptied, 1)

            def read_output(G):
                act.wait_ge(pv_done, G * NB + NB)
                if not (isinstance(G, int) and G == 0):
                    act.wait_ge(recip_ready, G)
                act.activation(oT[:, :], ps_out[:, :], ACT.Copy).then_inc(oT_ready, 1)

            for n in range(2):
                for kind in ("xa", "q", "k", "v"):
                    if (kind, n) == ("q", 0):
                        act.wait_ge(consts_ready, 3)
                    empty(kind, n)
                if n == 0:
                    place_values(0, 0)

            def body(b, par):
                for g in range(GROUPS):
                    G = b * GROUPS + g
                    for k in range(GROUP * NB):
                        m, j = k // GROUP, k % GROUP
                        act.wait_ge(scoresT_ready, G * 16 + (k + 1))
                        if j == 0 and not (isinstance(b, int) and G * NB + m < PROBS_RING):
                            act.wait_ge(pv_done, G * NB + (m + 1 - PROBS_RING))
                        act.activation(probs[:, m, j, :], ps_scoresT[:, bank(g, par, k)[0], :], ACT.Exp).then_inc(probs_ready, 1)
                        if k == 3 and not at_start(b, g):
                            read_output(G - 1)
                        if g == 0 and k == 13 and has_next(b):
                            place_values(b + 1, 1 - par)
                        if prepares(b):
                            kind = {(2, 1): "xa", (2, 13): "q", (3, 1): "k", (3, 13): "v"}.get((g, k))
                            if kind:
                                empty(kind, b + 2)

            batches(act, body)
            read_output(G_ALL - 1)

        @block.vector
        def _(dve):
            dve.memset(v_one[:, :, :, :, DH:DH + 1], 1.0)
            dve.memset(ps_out[:, :], 0.0).then_inc(consts_ready, 1)
            dve.wait_ge(params_loaded, 16 * PARAM_DMAS)
            dve.tensor_copy(wp_hi[:, :, :], wp_raw[:, :, :]).then_inc(consts_ready, 1)
            dve.wait_ge(consts_ready, 2)
            dve.tensor_scalar(bq_scaled[:, :], vec[:, 2:3], SCALE, None, ALU.mult)
            dve.tensor_tensor(wp_lo[:, :, :], wp_raw[:, :, :], wp_hi[:, :, :].bitcast(F32),
                              ALU.subtract).then_inc(consts_ready, 1)

            def round_xa(n):
                dve.wait_ge(misc_emptied, use_of("xa", n) + 1)
                if not (isinstance(n, int) and n == 0):
                    dve.wait_ge(misc_filled, use_of("v", n - 1) + 1)
                dve.tensor_copy(xaT_hi[:, :], xaT[:, :]).then_inc(xa_hi_ready, 1)

            def round_terms(kind, n, par):
                dve.wait_ge(misc_emptied, use_of(kind, n) + 1)
                src = {"q": qT, "k": kT}[kind]
                if kind == "q":
                    dst = q_terms[:, par, HI_SLOTS_Q[0]:HI_SLOTS_Q[1] + 1, :]
                else:
                    dst = k_terms[:, par, HI_SLOTS_K[0]:HI_SLOTS_K[1] + 1:2, :]
                twice = src[:, :].rearrange("p (o t) -> p o t", o=1).broadcast_to([P, 2, T])
                dve.tensor_copy(dst, twice).then_inc(hi_terms, 1)

            def take_maxima(G, g, par, k):
                dve.wait_ge(scores_ready, G * 16 + (k + 1))
                dve.tensor_reduce(maxima[:, g % 2, k:k + 1], ps_scores[:, bank(g, par, k)[0], :], AX_X,
                                  ALU.max).then_inc(maxima_ready, 1)

            def make_shift(use, par):
                dve.wait_ge(misc_filled, use + 1)
                dve.tensor_scalar(shift[:, par, :], ps_misc[0:GROUP * NB, 0:P], -1.0, None,
                                  ALU.mult).then_inc(misc_emptied, 1)

            def finish_output(use, G, g, par, b_before=None):
                dve.wait_ge(misc_filled, use + 1)
                dve.wait_ge(misc_emptied, use)
                if g == 0 and not (isinstance(G, int) and G < 2 * GROUPS):
                    added = G // GROUPS - 1 if isinstance(G, int) else b_before
                    dve.wait_ge(total_step, added * TOTAL)
                o = ps_misc[:, :].rearrange("p (n j r) -> p n j r", n=NB, r=ROWS)
                dve.reciprocal(recip[:, :, :], o[:, :, :, DH]).then_inc(recip_ready, 1)
                dve.wait_ge(recip_ready, G + 1)
                dst = attn[:, par, :, g * GROUP * DH:(g + 1) * GROUP * DH].rearrange("p n (j d) -> p n j d", d=DH)
                rb = recip[:, :, :].rearrange("p n (j o) -> p n j o", o=1).broadcast_to([P, NB, GROUP, DH])
                dve.tensor_tensor(dst, o[:, :, :, 0:DH], rb, ALU.mult).then_inc(misc_emptied, 1)

            round_xa(0)
            dve.memset(q_stack[:, 0].bitcast(F32), 0.0).then_inc(dve_cleared, 1)
            round_terms("q", 0, 0)
            round_terms("k", 0, 0)
            dve.memset(q_stack[:, 1].bitcast(F32), 0.0).then_inc(dve_cleared, 1)
            for G in range(2):
                for k in range(GROUP * NB):
                    take_maxima(G, G, 0, k)
                    if (G, k) == (1, 3):
                        make_shift(LEAD_M, 0)
                    if (G, k) == (1, 7):
                        round_xa(1)
                    if (G, k) == (1, 12):
                        round_terms("q", 1, 1)
                    if (G, k) == (1, 15):
                        round_terms("k", 1, 1)

            def body(b, par):
                for g in range(GROUPS):
                    G = b * GROUPS + g
                    ahead = not isinstance(b, int) or G + 2 < G_ALL
                    for k in range(GROUP * NB):
                        if ahead:
                            take_maxima(G + 2, (g + 2) % GROUPS, par if g < 2 else 1 - par, k)
                        if k == 4 and not at_end(b, g):
                            make_shift(use_m(b, g), (g + 1) % 2)
                        if k == 9 and not at_start(b, g):
                            finish_output(use_t(b, g), G - 1, (g - 1) % GROUPS, par if g else 1 - par, b - 1)
                        if prepares(b):
                            if (g, k) == (2, 2):
                                round_xa(b + 2)
                            if (g, k) == (2, 15):
                                round_terms("q", b + 2, par)
                            if (g, k) == (3, 4):
                                round_terms("k", b + 2, par)

            batches(dve, body)
            finish_output(misc_before(B - 1, GROUPS - 1) + 1, G_ALL - 1, GROUPS - 1, (B - 1) % 2)


def route_block(nc, env):
    x, router, router_bias, rank, tile_no, tri, ident_in = (
        env[k] for k in ("x", "router", "router_bias", "rank", "tile_no", "tri", "ident_in"))
    B, T, D, NB, TB, E, TILES = (env[k] for k in ("B", "T", "D", "NB", "TB", "E", "TILES"))
    slots_dram, ident, xn, r2, logits_all, rank8, numbers, before, ones, zeros, SPARE, SLOTS = (
        env[k] for k in ("slots_dram", "ident", "xn", "r2", "logits", "rank8", "numbers", "before", "ones", "zeros",
                         "SPARE", "SLOTS"))
    experts, shared_w, NE, HID, xnT = (env[k] for k in ("experts", "shared_w", "NE", "HID", "xnT"))
    CHUNK = 4
    CHUNKS = B // CHUNK
    CB = CHUNK * NB
    ROW = P // CHUNK

    with ExitStack() as ctx:
        def sb(name, shape, dt=F32):
            return ctx.enter_context(nc.sbuf_tensor(name, shape, dt))

        def sem(name):
            return ctx.enter_context(nc.semaphore(name))

        w_router = sb("w_router", [P, E])
        bias8 = sb("bias8", [P, E])
        minus_half = sb("minus_half", [P, CB])
        bn = sb("bn", [P, 2, NB, 6])
        moments = sb("moments", [P, TB, 2])
        coef = sb("coef", [P, 6, TB])
        shared_raw = sb("shared_raw", [P, NE - E, 3 * HID])
        logitsT = sb("logitsT", [P, T])

        ps_turn = ctx.enter_context(nc.psum_tensor("ps_turn", [P, 2, T], F32))
        ps_logitsT = ctx.enter_context(nc.psum_tensor("ps_logitsT", [P, T], F32))
        ps_logits = ctx.enter_context(nc.psum_tensor("ps_logits", [P, T], F32))

        params = sem("r_params")
        x_loaded = [sem(f"r_x_loaded{n}") for n in range(B)]
        consts = sem("r_consts")
        cleared = sem("r_cleared")
        bn_done = sem("bn_done")
        moments_ready = sem("moments_ready")
        coef_step = sem("coef_step")
        normed = [sem("normed_dve"), sem("normed_act")]
        turned = sem("r_turned")
        xnT_ready = sem("xnT_ready")
        logitsT_done = sem("logitsT_done")
        logitsT_read = sem("logitsT_read")
        logits_done = sem("logits_done")
        logits_read = sem("logits_read")
        zeroed = sem("zeroed")
        shared_loaded = sem("shared_loaded")
        shared_hi_ready = sem("shared_hi_ready")
        block = ctx.enter_context(nc.Block())
        PARAMS = 6
        COEF = 7

        @block.sync
        def _(sp):
            for n in range(B):
                sp.dma_start(xn[:, n * NB:(n + 1) * NB, :],
                             x[n].rearrange("(n p) d -> p n d", p=P)).then_inc(x_loaded[n], 16)
                if n == 1:
                    sp.dma_start(ident[:, :], ident_in).then_inc(params, 16)
                    sp.dma_start(w_router[:, :], router).then_inc(params, 16)
                    sp.dma_start(bias8[:, :], router_bias.partition_broadcast(P)).then_inc(params, 16)
                    sp.dma_start(rank8[:, :], rank.partition_broadcast(P)).then_inc(params, 16)
                    sp.dma_start(numbers[:, :], tile_no[0:TILES].partition_broadcast(P)).then_inc(params, 16)
                    sp.dma_start(before[:, :], tri).then_inc(params, 16)
            sp.dma_start(shared_raw[:, :, :], experts[:, E:NE, :]).then_inc(shared_loaded, 16)
            sp.wait_ge(consts, 2)
            for i in range(SPARE):
                first = SLOTS - (SPARE - i) * T
                sp.dma_start(slots_dram[first:first + T].rearrange("(p n) d -> p n d", p=P),
                             zeros[:, :, :]).then_inc(zeroed, 16)
            sp.wait_ge(zeroed, 16 * SPARE)

        @block.gpsimd
        def _(pool):
            pool.memset(ones[:, :], 1.0)
            pool.memset(minus_half[:, :], -0.5).then_inc(consts, 1)
            pool.memset(zeros[:, :, :], 0.0).then_inc(consts, 1)
            pool.wait_ge(consts, 1)
            for c in range(CHUNKS):
                t = slice(c * CB, (c + 1) * CB)
                pool.wait_ge(coef_step, c * COEF + 1)
                pool.tensor_tensor(coef[:, 1, t], coef[:, 0, t], minus_half[:, :], ALU.pow).then_inc(coef_step, 1)
                if c == 2:
                    pool.wait_ge(shared_hi_ready, 1)
                    pool.tensor_tensor(shared_w[:, 0, 1], shared_raw[:, :, :], shared_w[:, 0, 0].bitcast(F32), ALU.subtract)
                pool.wait_ge(coef_step, c * COEF + 6)
                pool.tensor_tensor(r2[:, t], coef[:, 5, t], minus_half[:, :], ALU.pow).then_inc(coef_step, 1)

        @block.tensor
        def _(pe):
            def logits(c):
                pe.wait_ge(xnT_ready, (c + 1) * CHUNK)
                if c:
                    pe.wait_ge(logitsT_read, c)
                for j in range(CHUNK):
                    mm = pe.matmul(ps_logitsT[j * ROW:j * ROW + E, :], w_router[:, :], xnT[:, c * CHUNK + j, :],
                                   start=True, stop=True, tile_position=(0, j * ROW))
                mm.then_inc(logitsT_done, 1)

            def turn_logits(c):
                pe.wait_ge(logitsT_read, c + 1)
                if c:
                    pe.wait_ge(logits_read, c)
                for t in range(NB):
                    mm = pe.transpose(ps_logits[:, t * P:(t + 1) * P], logitsT[:, t * P:(t + 1) * P], ident[:, :])
                mm.then_inc(logits_done, 1)

            pe.wait_ge(params, 16 * PARAMS)
            pe.wait_ge(cleared, 1)
            for n in range(B):
                for part in normed:
                    pe.wait_ge(part, (n + 1) * NB // 2)
                if n >= 2:
                    pe.wait_ge(xnT_ready, n - 1)
                for t in range(NB):
                    mm = pe.transpose(ps_turn[:, n % 2, t * P:(t + 1) * P], xn[:, n * NB + t, :], ident[:, :])
                mm.then_inc(turned, 1)
                if n and n % CHUNK == 0:
                    logits(n // CHUNK - 1)
                if n > CHUNK and n % CHUNK == 1:
                    turn_logits(n // CHUNK - 1)
            logits(CHUNKS - 1)
            turn_logits(CHUNKS - 1)

        @block.scalar
        def _(act):
            def normalise(n):
                act.wait_ge(coef_step, n // CHUNK * COEF + 3)
                for t in range(n * NB + NB // 2, (n + 1) * NB):
                    act.activation(xn[:, t, :], xn[:, t, :], ACT.Identity, bias=coef[:, 2, t:t + 1],
                                   scale=coef[:, 1, t:t + 1]).then_inc(normed[1], 1)

            def read_turned(n):
                act.wait_ge(turned, n + 1)
                act.activation(xnT[:, n, :], ps_turn[:, n % 2, :],
                               ACT.Copy).then_inc(xnT_ready, 1)

            for n in range(B + 1):
                if n < B:
                    normalise(n)
                if n:
                    read_turned(n - 1)
                if n == CHUNK:
                    act.wait_ge(shared_loaded, 16)
                    act.activation(shared_w[:, 0, 0], shared_raw[:, :, :], ACT.Copy).then_inc(shared_hi_ready, 1)

        @block.vector
        def _(dve):
            dve.memset(ps_logitsT[:, :], 0.0).then_inc(cleared, 1)
            dve.wait_ge(cleared, 1)

            def statistics(n):
                dve.wait_ge(x_loaded[n], 16)
                if n >= 2:
                    dve.wait_ge(moments_ready, (n - 1) * NB)
                for t in range(NB):
                    dve.bn_stats(bn[:, n % 2, t, :], xn[:, n * NB + t, :]).then_inc(bn_done, 1)

            def aggregate(n):
                for t in range(NB):
                    dve.wait_ge(bn_done, n * NB + t + 1)
                    dve.bn_aggr(moments[:, n * NB + t, :], bn[:, n % 2, t, :]).then_inc(moments_ready, 1)

            def parts(c):
                t = slice(c * CB, (c + 1) * CB)
                return moments[:, t, 0], moments[:, t, 1], *(coef[:, k, t] for k in range(6))

            def variance(c):
                mean, var, ve, r, bias, vr, vrr, ve2 = parts(c)
                dve.wait_ge(moments_ready, (c + 1) * CB)
                dve.tensor_scalar(ve, var, EPS, None, ALU.add).then_inc(coef_step, 1)

            def coefficients(c):
                mean, var, ve, r, bias, vr, vrr, ve2 = parts(c)
                done = c * COEF
                dve.wait_ge(coef_step, done + 2)
                dve.scalar_tensor_tensor(out=bias, in0=mean, scalar=-1.0, in1=r,
                                         op0=ALU.mult, op1=ALU.mult).then_inc(coef_step, 1)
                dve.wait_ge(coef_step, done + 3)
                dve.tensor_tensor(vr, var, r, ALU.mult).then_inc(coef_step, 1)
                dve.wait_ge(coef_step, done + 4)
                dve.tensor_tensor(vrr, vr, r, ALU.mult).then_inc(coef_step, 1)
                dve.wait_ge(coef_step, done + 5)
                dve.tensor_scalar(ve2, vrr, EPS, None, ALU.add).then_inc(coef_step, 1)

            def normalise(n):
                dve.wait_ge(coef_step, n // CHUNK * COEF + 3)
                for t in range(n * NB, n * NB + NB // 2):
                    dve.tensor_scalar(xn[:, t, :], xn[:, t, :], coef[:, 1, t:t + 1], coef[:, 2, t:t + 1],
                                      ALU.mult, ALU.add).then_inc(normed[0], 1)

            def read_logitsT(c):
                dve.wait_ge(logitsT_done, c + 1)
                if c:
                    dve.wait_ge(logits_done, c)
                dve.tensor_copy(logitsT[:, :], ps_logitsT[:, :]).then_inc(logitsT_read, 1)

            def read_logits(c):
                dve.wait_ge(logits_done, c + 1)
                if c == 0:
                    dve.wait_ge(params, 16 * PARAMS)
                src = ps_logits[:, :].rearrange("p (t j r) -> p j t r", t=NB, j=CHUNK)[:, :, :, 0:E]
                dst = logits_all[:, c * CB:(c + 1) * CB, :].rearrange("p (j t) e -> p j t e", j=CHUNK)
                bias = bias8[:, :].rearrange("p (o u e) -> p o u e", o=1, u=1).broadcast_to([P, CHUNK, NB, E])
                dve.tensor_tensor(dst, src, bias, ALU.add).then_inc(logits_read, 1)

            for c in range(CHUNKS + 2):
                for j in range(CHUNK):
                    n = c * CHUNK + j
                    if c < CHUNKS:
                        statistics(n)
                        aggregate(n)
                    if 1 <= c <= CHUNKS:
                        if j == 1:
                            coefficients(c - 1)
                            normalise(n - CHUNK - 1)
                        if j:
                            normalise(n - CHUNK)
                    if c >= 2 and j == 2:
                        read_logitsT(c - 2)
                    if c >= 2 and j == 3:
                        read_logits(c - 2)
                if c < CHUNKS:
                    variance(c)


def shared_block(nc, env):
    B, T, D, NB, TB, E, TILES, REGION = (env[k] for k in ("B", "T", "D", "NB", "TB", "E", "TILES", "REGION"))
    xnT = env["xnT"]
    (x, xn, base_dram, slots_dram, rows_out, picks, tile_expert, tile_slot, logits, rank8, numbers, before, ones,
     zeros) = (env[k] for k in ("x", "xn", "base_dram", "slots_dram", "slots", "picks", "tile_expert", "tile_slot",
                                "logits", "rank8", "numbers", "before", "ones", "zeros"))
    CHUNK = 4
    CHUNKS = B // CHUNK
    CB = CHUNK * NB
    PARTS = 8
    STEPS = 20 + E
    BOTH, COUNTED = 12, 13 + E
    UNITS = 2 * env["HC"]
    FIRST_UNIT = 2
    PICK_UNITS = (CHUNKS - 1) * PARTS
    ALONE = -(-(FIRST_UNIT + PICK_UNITS + 9) // (2 * UNITS)) * 2
    TABLE = CHUNKS * STEPS

    with ExitStack() as ctx:
        def sb(name, shape, dt=F32):
            return ctx.enter_context(nc.sbuf_tensor(name, shape, dt))

        def sem(name):
            return ctx.enter_context(nc.semaphore(name))

        eq1, key1, sel1, rest, eq2, key2, sel2, both, upto, earlier, place, slot1, slot2 = (
            sb(name, [P, TB, E]) for name in ("eq1", "key1", "sel1", "rest", "eq2", "key2", "sel2", "both", "upto",
                                              "earlier", "place", "in_slot1", "in_slot2"))
        m1, k1, m2, k2, diff, e_diff, total, slot_no1, slot_no2 = (sb(name, [P, TB]) for name in (
            "m1", "k1", "m2", "k2", "diff", "e_diff", "total_weight", "slot_no1", "slot_no2"))
        region, count, tiles, tiles_upto, slots_over, moved_by = (sb(name, [P, E]) for name in (
            "region", "count", "tiles", "tiles_upto", "slots_over", "moved_by"))
        slots = [sb(f"slot_in{k}", [P, TB], U32) for k in range(TOP_K)]
        moved = [sb(f"moved{k}", [P, TB]) for k in range(TOP_K)]
        first_free = sb("first_free", [P, E], U32)
        more_than = sb("more_than", [P, E, B])
        past = sb("past", [P, TILES, E])
        past_slots = sb("past_slots", [P, TILES, E])
        expert_no = sb("expert_no", [P, TILES])
        shift_of = sb("shift_of", [P, TILES])
        ps_place = ctx.enter_context(nc.psum_tensor("ps_place", [P, T], F32))

        step = sem("pick_step")
        region_ready = sem("region_ready")
        placed = sem("placed")
        exp_ready = sem("pick_exp_ready")
        weight_step = sem("weight_step")
        tails_cleared = sem("tails_cleared")
        totals = ps_place[:, CB * E:CB * E + E]

        def chunk_of(v, c):
            return v[:, c * CB:(c + 1) * CB]

        def by_token(v):
            return v.rearrange("p (t o) -> p t o", o=1).broadcast_to([P, v.shape[1], E])

        def by_expert(v, n):
            return v.rearrange("p (o e) -> p o e", o=1).broadcast_to([P, n, E])

        def begin_vector(dve):
            dve.tensor_scalar(region[:, :], rank8[:, :], float(-REGION), float(E * REGION),
                              ALU.mult, ALU.add).then_inc(region_ready, 1)

        def pick(dve, c, part):
            at = c * STEPS
            lg, q1, y1, s1, rs, q2, y2, s2, bo, up, ea, pl, o1, o2 = (chunk_of(v, c) for v in (
                logits, eq1, key1, sel1, rest, eq2, key2, sel2, both, upto, earlier, place, slot1, slot2))
            a1, b1, a2, b2, df = (chunk_of(v, c) for v in (m1, k1, m2, k2, diff))
            rank = by_expert(rank8[:, :], CB)
            if part == 0:
                if c:
                    dve.wait_ge(step, at)
                dve.tensor_reduce(a1, lg, AX_X, ALU.max).then_inc(step, 1)
                dve.wait_ge(step, at + 1)
                dve.tensor_tensor(q1, lg, by_token(a1), ALU.is_equal).then_inc(step, 1)
                dve.wait_ge(step, at + 2)
                dve.tensor_tensor(y1, q1, rank, ALU.mult).then_inc(step, 1)
            elif part == 1:
                dve.wait_ge(step, at + 3)
                dve.tensor_reduce(b1, y1, AX_X, ALU.max).then_inc(step, 1)
                dve.wait_ge(step, at + 4)
                dve.tensor_tensor(s1, y1, by_token(b1), ALU.is_equal).then_inc(step, 1)
                dve.wait_ge(step, at + 5)
                dve.scalar_tensor_tensor(out=rs, in0=s1, scalar=FAR_BELOW, in1=lg,
                                         op0=ALU.mult, op1=ALU.add).then_inc(step, 1)
            elif part == 2:
                dve.wait_ge(step, at + 6)
                dve.tensor_reduce(a2, rs, AX_X, ALU.max).then_inc(step, 1)
                dve.wait_ge(step, at + 7)
                dve.tensor_tensor(q2, rs, by_token(a2), ALU.is_equal).then_inc(step, 1)
                dve.wait_ge(step, at + 8)
                dve.tensor_tensor(y2, q2, rank, ALU.mult).then_inc(step, 1)
            elif part == 3:
                dve.wait_ge(step, at + 9)
                dve.tensor_reduce(b2, y2, AX_X, ALU.max).then_inc(step, 1)
                dve.wait_ge(step, at + 10)
                dve.tensor_tensor(s2, y2, by_token(b2), ALU.is_equal).then_inc(step, 1)
                dve.wait_ge(step, at + 11)
                dve.tensor_tensor(bo, s1, s2, ALU.add).then_inc(step, 1)
            elif part == 4:
                dve.wait_ge(step, at + BOTH)
                for e in range(E):
                    start = upto[:, c * CB - 1, e:e + 1] if c else 0.0
                    dve.tensor_tensor_scan(up[:, :, e], ones[:, 0:CB], bo[:, :, e], start,
                                           ALU.mult, ALU.add).then_inc(step, 1)
                dve.wait_ge(step, at + (BOTH + E))
                dve.tensor_tensor(ea, up, bo, ALU.subtract).then_inc(step, 1)
            elif part == 7:
                dve.wait_ge(placed, c + 1)
                dve.wait_ge(region_ready, 1)
                dve.tensor_tensor(pl, ps_place[:, 0:CB * E].rearrange("p (t e) -> p t e", e=E),
                                  by_expert(region[:, :], CB), ALU.add).then_inc(step, 1)
                dve.wait_ge(step, at + (COUNTED + 1))
                dve.tensor_tensor(o1, pl, s1, ALU.mult).then_inc(step, 1)
                dve.tensor_tensor(o2, pl, s2, ALU.mult).then_inc(step, 1)
                dve.wait_ge(step, at + (COUNTED + 3))
                dve.tensor_reduce(chunk_of(slot_no1, c), o1, AX_X, ALU.add).then_inc(step, 1)
                dve.tensor_reduce(chunk_of(slot_no2, c), o2, AX_X, ALU.add).then_inc(step, 1)
                dve.wait_ge(step, at + (COUNTED + 5))
                dve.tensor_copy(chunk_of(slots[0], c), chunk_of(slot_no1, c)).then_inc(step, 1)
                dve.tensor_copy(chunk_of(slots[1], c), chunk_of(slot_no2, c)).then_inc(step, 1)

        def table(dve, part):
            at = TABLE
            if part == 0:
                dve.wait_ge(placed, CHUNKS + 1)
                dve.tensor_scalar(count[:, :], totals, 1.0 / T, None, ALU.mult).then_inc(step, 1)
                dve.tensor_tensor(first_free[:, :], totals, region[:, :], ALU.add).then_inc(step, 1)
                dve.wait_ge(step, at + 2)
                dve.tensor_tensor(more_than[:, :, :],
                                  count[:, :].rearrange("p (e o) -> p e o", o=1).broadcast_to([P, E, B]),
                                  numbers[:, 0:B].rearrange("p (o n) -> p o n", o=1).broadcast_to([P, E, B]),
                                  ALU.is_gt).then_inc(step, 1)
                dve.wait_ge(step, at + 3)
                dve.tensor_reduce(tiles[:, :], more_than[:, :, :], AX_X, ALU.add).then_inc(step, 1)
            elif part == 1:
                dve.wait_ge(step, at + 4)
                dve.tensor_tensor_scan(tiles_upto[:, :], ones[:, 0:E], tiles[:, :], 0.0,
                                       ALU.mult, ALU.add).then_inc(step, 1)
                dve.tensor_scalar(slots_over[:, :], tiles[:, :], float(-T), float(REGION),
                                  ALU.mult, ALU.add).then_inc(step, 1)
                dve.wait_ge(step, at + 6)
                dve.tensor_tensor(past[:, :, :], by_expert(tiles_upto[:, :], TILES), by_token(numbers[:, :]),
                                  ALU.is_le).then_inc(step, 1)
            elif part == 2:
                dve.wait_ge(step, at + 7)
                dve.tensor_reduce(expert_no[:, :], past[:, :, :], AX_X, ALU.add).then_inc(step, 1)
                dve.tensor_tensor(past_slots[:, :, :], past[:, :, :], by_expert(slots_over[:, :], TILES),
                                  ALU.mult).then_inc(step, 1)
                dve.wait_ge(step, at + 9)
                dve.tensor_reduce(shift_of[:, :], past_slots[:, :, :], AX_X, ALU.add).then_inc(step, 1)
            elif part == 3:
                dve.wait_ge(step, at + 10)
                dve.tensor_scalar(tile_expert[:, :], expert_no[:, :], float(E - 1), None, ALU.min).then_inc(step, 1)
                dve.scalar_tensor_tensor(out=tile_slot[:, :], in0=numbers[:, :], scalar=float(T), in1=shift_of[:, :],
                                         op0=ALU.mult, op1=ALU.add).then_inc(step, 1)
                dve.tensor_tensor(diff[:, :], m2[:, :], m1[:, :], ALU.subtract).then_inc(step, 1)

        def rows_of_outputs(dve, part):
            at = TABLE + 13
            if part == 0:
                dve.wait_ge(step, at)
                dve.scalar_tensor_tensor(out=moved_by[:, :], in0=tiles_upto[:, :], scalar=float(T), in1=slots_over[:, :],
                                         op0=ALU.mult, op1=ALU.add).then_inc(step, 1)
                dve.wait_ge(step, at + 1)
                dve.tensor_tensor(moved_by[:, :], moved_by[:, :], region[:, :], ALU.subtract).then_inc(step, 1)
            elif part == 1:
                dve.wait_ge(step, at + 2)
                dve.tensor_tensor(slot1[:, :, :], sel1[:, :, :], by_expert(moved_by[:, :], TB), ALU.mult).then_inc(step, 1)
                dve.tensor_tensor(slot2[:, :, :], sel2[:, :, :], by_expert(moved_by[:, :], TB), ALU.mult).then_inc(step, 1)
            elif part == 2:
                for k, products in enumerate((slot1, slot2)):
                    dve.wait_ge(step, at + 3 + k)
                    dve.tensor_reduce(moved[k][:, :], products[:, :, :], AX_X, ALU.add).then_inc(step, 1)
            elif part == 3:
                for k, slot_no in enumerate((slot_no1, slot_no2)):
                    dve.wait_ge(step, at + 5 + k)
                    dve.scalar_tensor_tensor(out=rows_out[k][:, :], in0=moved[k][:, :], scalar=float(-REGION),
                                             in1=slot_no[:, :], op0=ALU.add, op1=ALU.add).then_inc(step, 1)

        def while_vector(dve, n, u):
            if not isinstance(n, int):
                return
            unit = n * UNITS + u
            if unit == -1:
                for part in range(PARTS - 1):
                    pick(dve, 0, part)
            if unit == 1:
                pick(dve, 0, PARTS - 1)
            unit -= FIRST_UNIT
            if 0 <= unit < PICK_UNITS:
                pick(dve, 1 + unit // PARTS, unit % PARTS)
            part = unit - PICK_UNITS - 1
            if 0 <= part < 4:
                table(dve, part)
            elif 4 <= part < 8:
                rows_of_outputs(dve, part - 4)

        def count_before(pe, c):
            pe.wait_ge(step, c * STEPS + COUNTED)
            flat = ps_place[:, 0:CB * E]
            pe.matmul(flat, before[:, :], chunk_of(both, c).rearrange("p t e -> p (t e)"), start=True, stop=False)
            pe.matmul(flat, ones[:, :], chunk_of(earlier, c).rearrange("p t e -> p (t e)"),
                      start=False, stop=True).then_inc(placed, 1)

        def while_tensor(pe, n, u):
            if not isinstance(n, int) or n < 0:
                return
            unit = n * UNITS + u
            if unit == 1:
                count_before(pe, 0)
            unit -= FIRST_UNIT
            if 0 <= unit < PICK_UNITS and unit % PARTS == 6:
                count_before(pe, 1 + unit // PARTS)
            if unit == PICK_UNITS:
                pe.wait_ge(step, TABLE)
                pe.matmul(totals, ones[:, :], upto[:, TB - 1, :], start=True, stop=True).then_inc(placed, 1)

        def while_sync(sp, n):
            if isinstance(n, int) and n in (ALONE - 2, ALONE - 1):
                sp.wait_ge(step, TABLE + 2)
                half = E // 2
                for e in range((n - ALONE + 2) * half, (n - ALONE + 3) * half):
                    row = sp.value_load(first_free[0:1, e:e + 1], min_val=0, max_val=E * REGION - T)
                    sp.dma_start(slots_dram[bass.ds(row, T)].rearrange("(p n) d -> p n d", p=P),
                                 zeros[:, :, :]).then_inc(tails_cleared, 16)

        def scatter(pool, scattered):
            for c in range(CHUNKS):
                pool.wait_ge(step, (c + 1) * STEPS)
                for t in range(c * CB, (c + 1) * CB):
                    for k in range(TOP_K):
                        pool.indirect_dma_start(slots_dram,
                                                bass.IndirectOffsetOnAxis(ap=slots[k][:, t:t + 1], axis=0),
                                                xn[:, t, :], None).then_inc(scattered, 16)
            pool.wait_ge(tails_cleared, 16 * E)
            pool.wait_ge(scattered, 16 * TOP_K * TB)

        def end_scalar(act):
            act.wait_ge(step, TABLE + 13)
            act.activation(e_diff[:, :], diff[:, :], ACT.Exp).then_inc(exp_ready, 1)

        def end_vector(dve):
            dve.wait_ge(exp_ready, 1)
            dve.tensor_scalar(total[:, :], e_diff[:, :], 1.0, None, ALU.add).then_inc(weight_step, 1)
            dve.wait_ge(weight_step, 1)
            dve.reciprocal(picks[0][:, :], total[:, :]).then_inc(weight_step, 1)
            dve.wait_ge(weight_step, 2)
            dve.tensor_tensor(picks[1][:, :], e_diff[:, :], picks[0][:, :], ALU.mult).then_inc(weight_step, 1)

        def tokens(sp, n):
            return xnT[:, bass.ds(n, 1), :].rearrange("p o (n d) -> p (o n) d", n=NB)

        def residual(n):
            src = x[n] if isinstance(n, int) else x[bass.ds(n, 1)].rearrange("o t d -> (o t) d")
            return src.rearrange("(n p) d -> p n d", p=P)

        def result(sp, n):
            return base_dram[n] if isinstance(n, int) else base_dram[bass.ds(n, 1)].rearrange("o p n d -> (o p) n d")

        feed_forward(nc, env, "s", B, 2, tokens, result, residual=residual, lead=ALONE,
                     turned=True, meanwhile={"sync": while_sync, "vector": while_vector, "tensor": while_tensor, "gpsimd": scatter,
                                "begin_vector": begin_vector, "end_scalar": end_scalar,
                                "end_vector": end_vector})


def routed_block(nc, env):
    slots_dram, routed_dram, T, tile_slot, SLOTS = (
        env[k] for k in ("slots_dram", "routed_dram", "T", "tile_slot", "SLOTS"))

    def tokens(sp, n):
        first = sp.value_load(tile_slot[0:1, bass.ds(n, 1)], min_val=0, max_val=SLOTS - T)
        return slots_dram[bass.ds(first, T)].rearrange("(n p) d -> p n d", p=P)

    def result(sp, n):
        return routed_dram[bass.ds(n * T, T)].rearrange("(n p) d -> p n d", p=P)

    feed_forward(nc, env, "t", env["TILES"], 1, tokens, result, by_tile=True)


def feed_forward(nc, env, name, rounds, per_round, tokens, result, residual=None, meanwhile=None, by_tile=False,
                 lead=None, turned=False):
    T, D, NB, E, HID, HC = (env[k] for k in ("T", "D", "NB", "E", "HID", "HC"))
    experts, ident, tile_expert = (env[k] for k in ("experts", "ident", "tile_expert"))
    RING = 8
    U = per_round * HC
    R = RING // U
    LAG = 4
    SPLIT = 2
    D_LAG = LAG // U
    W_RING = 4 if by_tile else 1
    assert LAG % U == 0 and RING % U == 0 and SPLIT <= U and (not by_tile or R == W_RING)

    with ExitStack() as ctx:
        def sb(label, shape, dt):
            return ctx.enter_context(nc.sbuf_tensor(f"{name}_{label}", shape, dt))

        def sem(label):
            return ctx.enter_context(nc.semaphore(f"{name}_{label}"))

        def ps(label, shape):
            return ctx.enter_context(nc.psum_tensor(f"{name}_{label}", shape, F32))

        if by_tile:
            w_raw = sb("w_raw", [P, 2, per_round, 3 * HID], F32)
            w = sb("w", [P, W_RING, 2, per_round, 3 * HID], F32R)
        else:
            w = env["shared_w"]
        xt = sb("xt", [P, 2, NB, D], F32)
        x_hi = sb("x_hi", [P, 2, T], F32R)
        x_lo = sb("x_lo", [P, 2, T], F32R)
        gate = sb("gate", [P, RING, T], F32)
        prod = sb("prod", [P, RING, T], F32)
        p_hi = sb("p_hi", [P, RING, T], F32R)
        p_lo = sb("p_lo", [P, RING, T], F32R)
        res = sb("res", [P, 2, NB, D], F32)
        yT = sb("yT", [P, T], F32)
        y_out = sb("y_out", [P, 2, NB, D], F32)
        ps_h1 = ps("ps_h1", [P, 2, T])
        ps_h3 = ps("ps_h3", [P, 2, T])
        Y_BANKS = 1 if meanwhile else 2
        ps_y = ps("ps_y", [P, Y_BANKS, T])
        ps_in = ps("ps_in", [P, T])
        ps_out = ps("ps_out", [P, T])

        w_loaded = [sem("w_loaded0"), sem("w_loaded1")]
        w_hi_ready = sem("w_hi_ready")
        w_lo_ready = sem("w_lo_ready")
        xt_loaded = [sem("xt_loaded0"), sem("xt_loaded1")]
        res_loaded = [sem("res_loaded0"), sem("res_loaded1")]
        x_turned = sem("x_turned")
        x_hi_ready = sem("x_hi_ready")
        x_lo_ready = sem("x_lo_ready")
        h1_ready = sem("h1_ready")
        h3_ready = sem("h3_ready")
        gate_ready = sem("gate_ready")
        prod_ready = sem("prod_ready")
        p_hi_ready = sem("p_hi_ready")
        p_lo_ready = sem("p_lo_ready")
        down_done = sem("down_done")
        yT_ready = sem("yT_ready")
        y_turned = sem("y_turned")
        y_ready = sem("y_ready")
        y_stored = [sem("y_stored0"), sem("y_stored1")]
        scattered = sem("scattered")
        block = ctx.enter_context(nc.Block())

        def each_round(eng, body, first=-1):
            last = rounds - R - rounds % R
            peeled = lead or 2 * R
            for n in range(first, peeled):
                body(n, n % R)
            with eng.Fori(peeled // R, last // R) as turn:
                for q in range(R):
                    body(turn * R + q, q)
            for n in range(last, rounds + D_LAG + 2):
                body(n, n % R)

        def exists(n):
            return not isinstance(n, int) or 0 <= n < rounds

        def columns(q):
            return xt[:, q % 2].rearrange("p n d -> p (n d)") if turned else ps_in[:, :]

        def later(n, k):
            return not isinstance(n, int) or n >= k

        def times(n, q, ring):
            return n // ring + 1 if isinstance(n, int) else (n - q % ring) // ring + 1

        @block.sync
        def _(sp):
            def load_tokens(n, q):
                src = tokens(sp, n)
                if later(n, 2):
                    sp.wait_ge(x_lo_ready if turned else x_turned, n - 1)
                sp.dma_start(xt[:, q % 2], src).then_inc(xt_loaded[q % 2], 16)

            def load_residual(n, q):
                if later(n, 2):
                    sp.wait_ge(y_ready, n - 1)
                sp.dma_start(res[:, q % 2], residual(n)).then_inc(res_loaded[q % 2], 16)

            def load_weights(n, q):
                e = sp.value_load(tile_expert[0:1, bass.ds(n, 1)], min_val=0, max_val=E - 1)
                if later(n, 2):
                    sp.wait_ge(w_lo_ready, n - 1)
                sp.dma_start(w_raw[:, q % 2, 0], experts[:, bass.ds(e, 1), :].rearrange("p o c -> p (o c)")
                             ).then_inc(w_loaded[q % 2], 16)

            def body(n, q):
                if by_tile and exists(n + 2):
                    load_weights(n + 2, (q + 2) % R)
                if exists(n + 2):
                    load_tokens(n + 2, (q + 2) % R)
                if residual and exists(n - D_LAG):
                    load_residual(n - D_LAG, (q - D_LAG) % R)
                if meanwhile:
                    meanwhile["sync"](sp, n)
                done = n - 2 - D_LAG
                if exists(done):
                    dst = result(sp, done)
                    sp.wait_ge(y_ready, done + 1)
                    sp.dma_start(dst, y_out[:, (q - D_LAG) % 2]).then_inc(y_stored[(q - D_LAG) % 2], 16)

            each_round(sp, body, -2)
            for k, stored in enumerate(y_stored):
                sp.wait_ge(stored, 16 * ((rounds + 1 - k) // 2))

        @block.gpsimd
        def _(pool):
            def split_weights(n, q):
                pool.wait_ge(w_hi_ready, n + 1)
                pool.tensor_tensor(w[:, q % W_RING, 1], w_raw[:, q % 2], w[:, q % W_RING, 0].bitcast(F32),
                                   ALU.subtract).then_inc(w_lo_ready, 1)

            if by_tile:
                def body(n, q):
                    if exists(n + 1):
                        split_weights(n + 1, (q + 1) % R)

                each_round(pool, body)
            else:
                meanwhile["gpsimd"](pool, scattered)

        @block.tensor
        def _(pe):
            def turn_in(n, q):
                pe.wait_ge(xt_loaded[q % 2], times(n, q, 2) * 16)
                if later(n, 1):
                    pe.wait_ge(x_lo_ready, n)
                for t in range(NB):
                    mm = pe.transpose(ps_in[:, t * P:(t + 1) * P], xt[:, q % 2, t, :], ident[:, :])
                mm.then_inc(x_turned, 1)

            def turn_out(n):
                pe.wait_ge(yT_ready, n + 1)
                if later(n, 1):
                    pe.wait_ge(y_ready, n)
                for t in range(NB):
                    mm = pe.transpose(ps_out[:, t * P:(t + 1) * P], yT[:, t * P:(t + 1) * P], ident[:, :])
                mm.then_inc(y_turned, 1)

            def up(n, q, u):
                e, hc = u // HC, u % HC
                N = n * U + u
                if u == 0:
                    pe.wait_ge(x_lo_ready, n + 1)
                    if by_tile:
                        pe.wait_ge(w_lo_ready, n + 1)
                for third, bank, ready in ((0, ps_h1[:, u % 2, :], h1_ready), (1, ps_h3[:, u % 2, :], h3_ready)):
                    if not (isinstance(N, int) and N < 2):
                        pe.wait_ge(prod_ready if third else gate_ready, N - 1)
                    cols = slice(third * HID + hc * P, third * HID + (hc + 1) * P)
                    w_hi, w_lo = (w[:, q % W_RING, k, e, cols] for k in range(2))
                    pe.matmul(bank, w_hi, x_hi[:, q % 2, :], start=True, stop=False)
                    pe.matmul(bank, w_hi, x_lo[:, q % 2, :], start=False, stop=False)
                    pe.matmul(bank, w_lo, x_hi[:, q % 2, :], start=False, stop=True).then_inc(ready, 1)

            def down(n, q, u):
                e, hc = u // HC, u % HC
                pe.wait_ge(p_lo_ready, n * U + (u + 1))
                if u == 0 and later(n, Y_BANKS):
                    pe.wait_ge(yT_ready, n + 1 - Y_BANKS)
                cols = slice(2 * HID + hc * P, 2 * HID + (hc + 1) * P)
                w_hi, w_lo = (w[:, q % W_RING, k, e, cols] for k in range(2))
                bank, r = ps_y[:, q % Y_BANKS, :], (q * U + u) % RING
                pe.matmul(bank, w_hi, p_hi[:, r, :], start=(u == 0), stop=False)
                pe.matmul(bank, w_hi, p_lo[:, r, :], start=False, stop=False)
                pe.matmul(bank, w_lo, p_hi[:, r, :], start=False, stop=(u == U - 1)).then_inc(down_done, 1)

            def body(n, q):
                for u in range(U):
                    if exists(n):
                        up(n, q, u)
                    if u == 0 and exists(n + 1) and not turned:
                        turn_in(n + 1, (q + 1) % R)
                    if u == U - 1 and exists(n - 1 - D_LAG):
                        turn_out(n - 1 - D_LAG)
                    if exists(n - D_LAG):
                        down(n - D_LAG, (q - D_LAG) % R, u)
                    if meanwhile:
                        meanwhile["tensor"](pe, n, u)

            each_round(pe, body)

        @block.scalar
        def _(act):
            def round_x(n, q):
                if turned:
                    act.wait_ge(xt_loaded[q % 2], times(n, q, 2) * 16)
                else:
                    act.wait_ge(x_turned, n + 1)
                if later(n, 2):
                    act.wait_ge(h3_ready, (n - 1) * U)
                act.activation(x_hi[:, q % 2, :], columns(q), ACT.Copy).then_inc(x_hi_ready, 1)

            def round_weights(n, q):
                act.wait_ge(w_loaded[q % 2], times(n, q, 2) * 16)
                if later(n, W_RING):
                    act.wait_ge(down_done, (n - (W_RING - 1)) * U)
                act.activation(w[:, q % W_RING, 0], w_raw[:, q % 2], ACT.Copy).then_inc(w_hi_ready, 1)

            def silu(n, q, u):
                N = n * U + u
                act.wait_ge(h1_ready, N + 1)
                if not (isinstance(N, int) and N < RING):
                    act.wait_ge(prod_ready, N - (RING - 1))
                act.activation(gate[:, (q * U + u) % RING, :], ps_h1[:, u % 2, :], ACT.Silu).then_inc(gate_ready, 1)

            def round_product(N, r):
                act.wait_ge(prod_ready, N + 1)
                if not (isinstance(N, int) and N < RING):
                    act.wait_ge(down_done, N - (RING - 1))
                act.activation(p_hi[:, r, :], prod[:, r, :], ACT.Copy).then_inc(p_hi_ready, 1)

            def read_y(n, q):
                act.wait_ge(down_done, n * U + U)
                if later(n, 1):
                    act.wait_ge(y_turned, n)
                act.activation(yT[:, :], ps_y[:, q % Y_BANKS, :], ACT.Copy).then_inc(yT_ready, 1)

            def body(n, q):
                for u in range(U):
                    if u == 0 and Y_BANKS == 1 and exists(n - 1 - D_LAG):
                        read_y(n - 1 - D_LAG, (q - 1 - D_LAG) % R)
                    if exists(n):
                        silu(n, q, u)
                    if u == 0 and by_tile and exists(n + 1):
                        round_weights(n + 1, (q + 1) % R)
                    if u == 0 and exists(n + 1):
                        round_x(n + 1, (q + 1) % R)
                    if u == 0 and Y_BANKS == 2 and exists(n - 1 - D_LAG):
                        read_y(n - 1 - D_LAG, (q - 1 - D_LAG) % R)
                    N = n * U + (u - SPLIT)
                    if not isinstance(n, int) or 0 <= N < rounds * U:
                        round_product(N, (q * U + u - SPLIT) % RING)

            each_round(act, body)
            if meanwhile:
                meanwhile["end_scalar"](act)

        @block.vector
        def _(dve):
            def split_x(n, q):
                dve.wait_ge(x_hi_ready, n + 1)
                dve.tensor_tensor(x_lo[:, q % 2, :], columns(q), x_hi[:, q % 2, :].bitcast(F32),
                                  ALU.subtract).then_inc(x_lo_ready, 1)

            def multiply(n, q, u):
                N = n * U + u
                r = (q * U + u) % RING
                dve.wait_ge(gate_ready, N + 1)
                dve.wait_ge(h3_ready, N + 1)
                if not (isinstance(N, int) and N < RING):
                    dve.wait_ge(p_lo_ready, N - (RING - 1))
                dve.tensor_tensor(prod[:, r, :], ps_h3[:, u % 2, :], gate[:, r, :], ALU.mult).then_inc(prod_ready, 1)

            def split_product(N, r):
                dve.wait_ge(p_hi_ready, N + 1)
                if not (isinstance(N, int) and N < RING):
                    dve.wait_ge(down_done, N - (RING - 1))
                dve.tensor_tensor(p_lo[:, r, :], prod[:, r, :], p_hi[:, r, :].bitcast(F32),
                                  ALU.subtract).then_inc(p_lo_ready, 1)

            def finish(n, q):
                dve.wait_ge(y_turned, n + 1)
                if later(n, 2):
                    dve.wait_ge(y_stored[q % 2], (times(n, q, 2) - 1) * 16)
                src = ps_out[:, :].rearrange("p (n d) -> p n d", d=D)
                if residual:
                    dve.wait_ge(res_loaded[q % 2], times(n, q, 2) * 16)
                    dve.tensor_tensor(y_out[:, q % 2], src, res[:, q % 2], ALU.add).then_inc(y_ready, 1)
                else:
                    dve.tensor_copy(y_out[:, q % 2], src).then_inc(y_ready, 1)

            def body(n, q):
                for u in range(U):
                    if exists(n):
                        multiply(n, q, u)
                    if u == 0 and exists(n + 1):
                        split_x(n + 1, (q + 1) % R)
                    N = n * U + (u - SPLIT)
                    if not isinstance(n, int) or 0 <= N < rounds * U:
                        split_product(N, (q * U + u - SPLIT) % RING)
                    if u == U - 1 and exists(n - 1 - D_LAG):
                        finish(n - 1 - D_LAG, (q - 1 - D_LAG) % R)
                    if meanwhile:
                        meanwhile["vector"](dve, n, u)

            if meanwhile:
                meanwhile["begin_vector"](dve)
            each_round(dve, body)
            if meanwhile:
                meanwhile["end_vector"](dve)


def kernel(**inputs):
    import numpy as np
    import concourse.bacc as bacc
    from concourse.bass_utils import run_bass_kernel_spmd as run

    a = {k.replace("L0_attn_", "a_").replace("L0_ffn_", "f_"): np.asarray(v) for k, v in inputs.items()}
    x = np.ascontiguousarray(a["a_x"])
    D = x.shape[2]

    def first_layer(w):
        return w.transpose(2, 0, 1)

    def second_layer(w):
        n, d, h = w.shape
        return w.reshape(n, d, h // 128, 128).transpose(3, 0, 2, 1).reshape(128, n, h)

    every = {k: np.concatenate([a["f_" + k], a["f_s" + k]]) for k in ("w1", "w3", "w2")}
    laid = {
        "x": x,
        "vecs": np.stack([a[k] for k in ("a_ln_g", "a_ln_b", "a_bq", "a_bk", "a_bv")], 1),
        "wqkv": np.stack([a["a_Wq"], a["a_Wk"], a["a_Wv"]], 1),
        "experts": np.concatenate(
            [first_layer(every["w1"]), first_layer(every["w3"]), second_layer(every["w2"])], 2),
        "router": a["f_router_w"].T,
        "router_bias": a["f_expert_bias"],
        "rank": np.arange(a["f_router_w"].shape[0], 0, -1).astype(np.float32),
        "tile_no": np.arange(2 * x.shape[0] + 8, dtype=np.float32),
        "tri": np.triu(np.ones((D, D), np.float32), 1),
        "ident_in": np.eye(D, dtype=np.float32),
    }
    nc = bacc.Bacc("TRN2", target_bir_lowering=False, num_devices=1)
    arrays, args = {}, []
    for name, v in laid.items():
        v = np.ascontiguousarray(v)
        arrays[f"{name}_dram"] = v
        args.append(nc.dram_tensor(f"{name}_dram", v.shape, mybir.dt.from_np(v.dtype), kind="ExternalInput").ap())
    args.append(nc.dram_tensor("out_dram", x.shape, F32, kind="ExternalOutput").ap())
    prenorm_attention_moe(nc, *args)
    r = run(nc, [arrays], core_ids=[0])
    return r.results[0]["out_dram"]
```
